# Optimizing a Trainium2 kernel written in Bass

```python
import numpy as np
import jax
import jax.numpy as jnp

def _softmax(x, axis=-1):
    return jax.nn.softmax(x, axis=axis)

def _gelu(x):
    return jax.nn.gelu(x, approximate=True)

def _silu(x):
    return jax.nn.silu(x)

def _sigmoid(x):
    return jax.nn.sigmoid(x)

def _layernorm(x, axis=-1, eps=1e-05):
    m = jnp.mean(x, axis=axis, keepdims=True)
    v = jnp.var(x, axis=axis, keepdims=True)
    return (x - m) / jnp.sqrt(v + eps)

def _scatter_add(tgt, idx, src, axis=0):
    return tgt.at[idx].add(src)

def _segment_sum(src, seg, n):
    return jax.ops.segment_sum(src, seg, n)
kernel_name = 'mk_seq_postln_d1_jaxref_r4_4d96b4'

def setup_inputs(seed: int=0):
    np.random.seed(seed)
    _w = jnp.asarray

    def _L0_attn_setup():
        import jax, jax.numpy as jnp
        import numpy as np
        N_HEADS = 16
        EPS = 1e-06

        def _feature_map(x):
            return jax.nn.elu(x) + 1.0
        key = jax.random.key(seed)
        k1, k2, k3 = jax.random.split(key, 3)
        B, S, D = (1, 512, 256)
        x = jax.random.normal(k1, (B, S, D), dtype=jnp.float32)
        causal_mask = jnp.tril(jnp.ones((S, S), dtype=bool))[None, None]
        W_qkv = jax.random.normal(k2, (D, 3 * D), dtype=jnp.float32) / np.sqrt(D)
        W_out = jax.random.normal(k3, (D, D), dtype=jnp.float32) / np.sqrt(D)
        return {'x': x, 'causal_mask': causal_mask, 'W_qkv': W_qkv, 'W_out': W_out}
    _L0_attn_in = _L0_attn_setup()

    def _L0_ffn_setup():
        import jax, jax.numpy as jnp
        import numpy as np
        D_MODEL = 256
        MLP_DIM = 1024
        N_EXPERTS = 8
        B, T = (4, 256)
        key = jax.random.key(seed)
        ks = jax.random.split(key, 7)
        scale_in = (1.0 / D_MODEL) ** 0.5
        scale_out = (1.0 / MLP_DIM) ** 0.5
        bound_g = (1.0 / D_MODEL) ** 0.5
        w_gate = jax.random.uniform(ks[0], (D_MODEL, N_EXPERTS), minval=-bound_g, maxval=bound_g, dtype=jnp.float32)
        b_gate = jax.random.uniform(ks[1], (N_EXPERTS,), minval=-bound_g, maxval=bound_g, dtype=jnp.float32)
        W1 = jax.random.uniform(ks[2], (N_EXPERTS, D_MODEL, MLP_DIM), minval=-scale_in, maxval=scale_in, dtype=jnp.float32)
        b1 = jnp.zeros((N_EXPERTS, MLP_DIM), dtype=jnp.float32)
        W2 = jax.random.uniform(ks[3], (N_EXPERTS, MLP_DIM, D_MODEL), minval=-scale_out, maxval=scale_out, dtype=jnp.float32)
        b2 = jnp.zeros((N_EXPERTS, D_MODEL), dtype=jnp.float32)
        x = jax.random.normal(ks[4], (B, T, D_MODEL), dtype=jnp.float32)
        return {'x': x, 'w_gate': w_gate, 'b_gate': b_gate, 'W1': W1, 'b1': b1, 'W2': W2, 'b2': b2}
    _L0_ffn_in = _L0_ffn_setup()
    _d = {'L0_attn_x': _L0_attn_in['x'], 'L0_attn_causal_mask': _L0_attn_in['causal_mask'], 'L0_attn_W_qkv': _L0_attn_in['W_qkv'], 'L0_attn_W_out': _L0_attn_in['W_out'], 'L0_ffn_w_gate': _L0_ffn_in['w_gate'], 'L0_ffn_b_gate': _L0_ffn_in['b_gate'], 'L0_ffn_W1': _L0_ffn_in['W1'], 'L0_ffn_b1': _L0_ffn_in['b1'], 'L0_ffn_W2': _L0_ffn_in['W2'], 'L0_ffn_b2': _L0_ffn_in['b2']}
    _x0 = _d['L0_attn_x']
    _d['L0_attn_x'] = jax.random.normal(jax.random.fold_in(jax.random.key(seed), 1), (4, 1024, 256), dtype=_x0.dtype)
    del _x0
    return _d

def reference(L0_attn_x, L0_attn_causal_mask, L0_attn_W_qkv, L0_attn_W_out, L0_ffn_w_gate, L0_ffn_b_gate, L0_ffn_W1, L0_ffn_b1, L0_ffn_W2, L0_ffn_b2):

    def _L0_attn_ref(x, causal_mask, W_qkv, W_out):
        import jax, jax.numpy as jnp
        import numpy as np
        N_HEADS = 16
        EPS = 1e-06

        def _feature_map(x):
            return jax.nn.elu(x) + 1.0
        B, S, D = x.shape
        H = N_HEADS
        hd = D // H
        qkv = x @ W_qkv
        q, k, v = jnp.split(qkv, 3, axis=-1)

        def to_heads(t):
            return t.reshape(B, S, H, hd).transpose(0, 2, 1, 3)
        q, k, v = (to_heads(q), to_heads(k), to_heads(v))
        phi_q = _feature_map(q)
        phi_k = _feature_map(k)
        k_cum = jnp.cumsum(phi_k, axis=2)
        kv = jnp.einsum('bhsi,bhsj->bhsij', phi_k, v)
        kv_cum = jnp.cumsum(kv, axis=2)
        numer = jnp.einsum('bhsi,bhsij->bhsj', phi_q, kv_cum)
        denom = jnp.einsum('bhsi,bhsi->bhs', phi_q, k_cum) + EPS
        attn_out = numer / denom[..., None]
        attn_out = attn_out.transpose(0, 2, 1, 3).reshape(B, S, D)
        return attn_out @ W_out

    def _L0_ffn_ref(x, w_gate, b_gate, W1, b1, W2, b2):
        import jax, jax.numpy as jnp
        import numpy as np
        D_MODEL = 256
        MLP_DIM = 1024
        N_EXPERTS = 8
        B, T = (4, 256)
        b, t, d = x.shape
        x_flat = x.reshape(b * t, d)
        logits = x_flat @ w_gate + b_gate
        probs = jax.nn.softmax(logits, axis=-1)
        route_p = jnp.max(probs, axis=-1)
        route_idx = jnp.argmax(probs, axis=-1)
        h = jnp.einsum('nd,edm->enm', x_flat, W1) + b1[:, None, :]
        h = jax.nn.relu(h)
        y = jnp.einsum('enm,emd->end', h, W2) + b2[:, None, :]
        n = b * t
        out = y[route_idx, jnp.arange(n)] * route_p[:, None]
        return out.reshape(b, t, d)
    x = L0_attn_x
    x = _layernorm(x + _L0_attn_ref(x, L0_attn_causal_mask, L0_attn_W_qkv, L0_attn_W_out), axis=-1)
    x = _layernorm(x + _L0_ffn_ref(x, L0_ffn_w_gate, L0_ffn_b_gate, L0_ffn_W1, L0_ffn_b1, L0_ffn_W2, L0_ffn_b2), axis=-1)
    return x

_drawn_inputs = setup_inputs


def setup_inputs(seed=0):
    import zlib

    import numpy as np

    out = dict(_drawn_inputs(seed))
    spreads = {'L0_ffn_b1': (0.0, 0.758), 'L0_ffn_b2': (0.0, 0.309)}
    factors = {'L0_ffn_b_gate': 4.312}
    for name, (base, spread) in spreads.items():
        noise = np.random.default_rng([zlib.crc32(name.encode()), seed]).standard_normal(out[name].shape)
        drawn = base * np.exp(spread * noise) if base else spread * noise
        out[name] = jnp.asarray(drawn.astype(out[name].dtype))
    for name, factor in factors.items():
        out[name] = (out[name] * factor).astype(out[name].dtype)
    return out
```

```python
from contextlib import ExitStack

import concourse.bass as bass
from concourse import mybir

ALU = mybir.AluOpType
ACT = mybir.ActivationFunctionType
F32 = mybir.dt.float32
BF16 = mybir.dt.bfloat16
I32 = mybir.dt.int32
U32 = mybir.dt.uint32
AX_X = mybir.AxisListType.X

P = 128
BATCH, SEQ, D = 4, 1024, 256
HEADS, HD = 16, 16
HV = HD + 1
E, F = 8, 1024
TOKENS = BATCH * SEQ
CHUNKS = TOKENS // P
BLOCKS = SEQ // P
KC = D // P
FC = F // P
TILES = CHUNKS + E - 1
HALF = HEADS // KC
LN_EPS = 1e-5
DEN_EPS = 1e-6
W1_ROW = KC * F + FC


def attention_moe(nc, x, xT, w_qkv, w_out, w_gate, b_gate, w1b, w2, b2, out):
    with ExitStack() as ctx:
        def sb(name, shape, dt=F32):
            return ctx.enter_context(nc.sbuf_tensor(name, shape, dt))

        def sem(name):
            return ctx.enter_context(nc.semaphore(name))

        x1_rows = nc.dram_tensor("x1_rows", (TOKENS, D), F32, kind="Internal").ap()
        x_rows = x.rearrange("b s d -> (b s) d")

        wqkv = sb("wqkv", [P, KC, 3 * D])
        wo = sb("wo", [P, KC, D])
        wg = sb("wg", [P, KC, E])
        bg = sb("bg", [P, E])
        w2s = sb("w2s", [P, E * FC * D])
        causal = sb("causal", [P, P])
        ident = sb("ident", [P, P])
        select = sb("select", [P, 4 * HV])
        diag = sb("diag", [P, HALF, HV])
        parity = sb("parity", [P, 2])
        iota_i = sb("iota_i", [P, P], I32)
        ln_power = sb("ln_power", [P, 1])
        ln_eps = sb("ln_eps", [P, 1])
        xt = sb("xt", [P, BATCH, KC, P])
        xn = sb("xn", [P, BATCH, D])
        expo = sb("expo", [P, 4 * P])
        relu = sb("relu", [P, 4 * P])
        phi = sb("phi", [P, 2, 4, P])
        kmask = sb("kmask", [P, 2, 2, KC, P])
        vext = sb("vext", [P, 2, HEADS, 32])
        kn = sb("kn", [P, 2, D])
        probs = sb("probs", [P, 4, 4, P])
        avt = sb("avt", [P, 4, P])
        state = sb("state", [P, BATCH, KC, HALF * HV])
        state_add = sb("state_add", [P, KC, HALF * HV])
        den = sb("den", [P, HEADS])
        rden = sb("rden", [P, HEADS])
        att = sb("att", [P, D])
        attT = sb("attT", [P, KC, P])
        z = sb("z", [P, 2, D])
        stats = sb("stats", [P, 6])
        mv = sb("mv", [P, 2, 2])
        veps = sb("veps", [P, 2])
        rstd = sb("rstd", [P, 2])
        x1 = sb("x1", [P, BATCH, D])
        x1T = sb("x1T", [P, KC, P])
        lg = sb("lg", [P, CHUNKS, E])
        lmax = sb("lmax", [P, CHUNKS])
        ex = sb("ex", [P, CHUNKS, E])
        esum = sb("esum", [P, CHUNKS])
        top_p = sb("top_p", [P, CHUNKS])
        rank8 = sb("rank8", [P, E])
        hit = sb("hit", [P, CHUNKS, E])
        first = sb("first", [P, CHUNKS])
        onehot = sb("onehot", [P, CHUNKS, E])
        onehot_b = sb("onehot_b", [P, CHUNKS * E], BF16)
        before_b = sb("before_b", [P, P], BF16)
        ones_b = sb("ones_b", [P, P], BF16)
        ones_row = sb("ones_row", [P, CHUNKS * E])
        total = sb("total", [P, E, CHUNKS])
        cum = sb("cum", [P, E, CHUNKS])
        count = sb("count", [P, E])
        estart = sb("estart", [P, E])
        steps = sb("steps", [P, CHUNKS])
        over = sb("over", [P, E, CHUNKS])
        ntile = sb("ntile", [P, E])
        tend = sb("tend", [P, E])
        shift = sb("shift", [P, E])
        base = sb("base", [P, E, CHUNKS])
        pick = sb("pick", [P, CHUNKS, E])
        slot = sb("slot", [P, CHUNKS])
        slot_i = sb("slot_i", [P, CHUNKS], I32)
        hi_i = sb("hi_i", [P, CHUNKS], I32)
        lo_i = sb("lo_i", [P, CHUNKS], I32)
        hi = sb("hi", [P, CHUNKS])
        lo = sb("lo", [P, CHUNKS])
        iota_p = sb("iota_p", [P, P])
        iota_b = sb("iota_b", [P, P], BF16)
        part1_i = sb("part1_i", [P, 1], I32)
        part1 = sb("part1", [P, 1])
        tval_i = sb("tval_i", [P, CHUNKS], I32)
        tval = sb("tval", [P, CHUNKS])
        lo_hot = sb("lo_hot", [P, CHUNKS, P], BF16)
        hi_hot = sb("hi_hot", [P, CHUNKS, TILES], BF16)
        mov = sb("mov", [P, CHUNKS, 5, TILES], BF16)
        p_part = sb("p_part", [P, 3, CHUNKS], BF16)
        p_rest = sb("p_rest", [P, 2, CHUNKS])
        slot_sb = sb("slot_sb", [P, 5, TILES])
        tok1 = sb("tok1", [P, TILES])
        gather_f = sb("gather_f", [P, TILES])
        scatter_f = sb("scatter_f", [P, TILES])
        gather_i = sb("gather_i", [P, TILES], U32)
        scatter_i = sb("scatter_i", [P, TILES], U32)
        slot_p = sb("slot_p", [P, TILES])
        slot_p2 = sb("slot_p2", [P, TILES])
        ended = sb("ended", [P, TILES, E])
        expert_f = sb("expert_f", [P, TILES])
        expert_i = sb("expert_i", [P, TILES], I32)
        w1s = sb("w1s", [P, 2, W1_ROW])
        b2s = sb("b2s", [P, 4, D])
        gidx = sb("gidx", [P, 4], U32)
        sidx = sb("sidx", [P, 2], U32)
        xg = sb("xg", [P, 4, D])
        xgT = sb("xgT", [P, 2, KC, P])
        hT = sb("hT", [P, 2, FC, P])
        yb = sb("yb", [P, D])
        z2 = sb("z2", [P, 2, D])
        stats2 = sb("stats2", [P, 6])
        mv2 = sb("mv2", [P, 2, 2])
        veps2 = sb("veps2", [P, 2])
        rstd2 = sb("rstd2", [P, 2])
        yo = sb("yo", [P, 2, D])

        bank = [ctx.enter_context(nc.psum_tensor(f"bank{i}", [P, 512], F32)) for i in range(8)]
        b_av, b_nat, b_kv, b_op = bank[0], bank[1], bank[2], bank[3]
        b_qk, b_vk, b_tr, b_lg = bank[4], bank[5], bank[6], bank[7]

        w_in = sem("w_in")
        w2_in = sem("w2_in")
        xt_in = [sem(f"xt_in{b}") for b in range(BATCH)]
        xn_in = [sem(f"xn_in{b}") for b in range(BATCH)]
        x1_out = [sem(f"x1_out{b}") for b in range(BATCH)]
        zeroed = sem("zeroed")
        consts = sem("consts")
        iotas = sem("iotas")
        vec_consts = sem("vec_consts")
        qk_done = sem("qk_done")
        v_done = sem("v_done")
        er_done = sem("er_done")
        v_evac = sem("v_evac")
        phi_done = sem("phi_done")
        kmask_done = sem("kmask_done")
        kn_done = sem("kn_done")
        kn_evac = sem("kn_evac")
        sc_done = sem("sc_done")
        probs_done = sem("probs_done")
        av_done = sem("av_done")
        av_evac = sem("av_evac")
        nat_done = sem("nat_done")
        den_done = sem("den_done")
        rden_done = sem("rden_done")
        att_done = sem("att_done")
        kv_done = sem("kv_done")
        kv_masked = sem("kv_masked")
        state_done = sem("state_done")
        attT_done = sem("attT_done")
        attT_evac = sem("attT_evac")
        op_done = sem("op_done")
        z_done = sem("z_done")
        stats_done = sem("stats_done")
        mv_done = sem("mv_done")
        veps_done = sem("veps_done")
        rstd_done = sem("rstd_done")
        x1_done = sem("x1_done")
        x1T_done = sem("x1T_done")
        x1T_evac = sem("x1T_evac")
        lg_done = sem("lg_done")
        route = sem("route")
        exp_done = sem("exp_done")
        count_done = sem("count_done")
        lo_hot_done = sem("lo_hot_done")
        mov_done = sem("mov_done")
        slots_done = sem("slots_done")
        experts_ready = sem("experts_ready")
        idx_ready = sem("idx_ready")
        w1_in = [sem(f"w1_in{b}") for b in range(2)]
        b2_in = [sem(f"b2_in{b}") for b in range(4)]
        xg_in = [sem(f"xg_in{b}") for b in range(4)]
        y_out = [sem(f"y_out{b}") for b in range(2)]
        first_gidx = sem("first_gidx")
        gidx_done = sem("gidx_done")
        sidx_done = sem("sidx_done")
        xgT_done = sem("xgT_done")
        xgT_evac = sem("xgT_evac")
        h_done = sem("h_done")
        h_act = sem("h_act")
        h_vec = sem("h_vec")
        y_done = sem("y_done")
        yb_done = sem("yb_done")
        z2_done = sem("z2_done")
        stats2_done = sem("stats2_done")
        mv2_done = sem("mv2_done")
        veps2_done = sem("veps2_done")
        rstd2_done = sem("rstd2_done")
        yo_done = sem("yo_done")

        block = ctx.enter_context(nc.Block())

        def groups(eng, body):
            body(0, True, False)
            with eng.Fori(1, BLOCKS - 1) as i:
                body(i, False, False)
            body(BLOCKS - 1, False, True)

        def tiles(eng, body):
            for j in range(4):
                body(j, j)
            with eng.Fori(1, TILES // 4 - 1) as k:
                for u in range(4):
                    body(4 * k + u, u)
            for j in range((TILES // 4 - 1) * 4, TILES):
                body(j, j % 4)

        @block.sync
        def _(sp):
            sp.dma_start(wqkv[:], w_qkv.rearrange("(c p) n -> p c n", p=P)).then_inc(w_in, 16)

            def load(t, i, b):
                sp.dma_start(xt[:, b], xT[bass.ds(i, 1), b].rearrange("a p c n -> (a p) c n")
                             ).then_inc(xt_in[b], 16)
                sp.dma_start(xn[:, b], x[b, bass.ds(i * P, P), :]).then_inc(xn_in[b], 16)

            for b in range(BATCH):
                load(b, 0, b)
                if b == 0:
                    sp.dma_start(wo[:], w_out.rearrange("(c p) n -> p c n", p=P)).then_inc(w_in, 16)
                    sp.dma_start(wg[:], w_gate.rearrange("(c p) n -> p c n", p=P)).then_inc(w_in, 16)
                    sp.dma_start(bg[:], b_gate.rearrange("(a e) -> a e", a=1).broadcast_to([P, E])
                                 ).then_inc(w_in, 16)
            for e in range(E):
                sp.dma_start(w2s[:, e * FC * D:(e + 1) * FC * D].rearrange("p (c n) -> p c n", c=FC),
                             w2[e].rearrange("(c p) n -> p c n", p=P)).then_inc(w2_in, 16)

            def store_x1(t, i, b):
                sp.wait_ge(x1_done, t + 1)
                sp.dma_start(x1_rows[bass.ds(b * SEQ + i * P, P), :], x1[:, b]
                             ).then_inc(x1_out[b], 16)

            with sp.Fori(1, BLOCKS) as i:
                for b in range(BATCH):
                    t = 4 * i + b
                    sp.wait_ge(v_done, t - 3)
                    sp.wait_ge(z_done, t - 3)
                    load(t, i, b)
                    store_x1(t - 4, i - 1, b)
            for b in range(BATCH):
                store_x1(4 * (BLOCKS - 1) + b, BLOCKS - 1, b)

            sp.wait_ge(experts_ready, 1)

            def load_w1(j, u):
                if not (isinstance(j, int) and j < 2):
                    sp.wait_ge(h_act, 4 * (j - 1))
                    sp.wait_ge(h_vec, 4 * (j - 1))
                e = sp.value_load(expert_i[0:1, bass.ds(j, 1)], min_val=0, max_val=E - 1)
                sp.dma_start(w1s[:, u % 2], w1b[bass.ds(e, 1)].rearrange("a p n -> (a p) n")
                             ).then_inc(w1_in[u % 2], 16)
                if not (isinstance(j, int) and j < 4):
                    sp.wait_ge(yb_done, j - 3)
                sp.dma_start(b2s[:, u % 4], b2[bass.ds(e, 1), :].broadcast_to([P, D])
                             ).then_inc(b2_in[u % 4], 16)

            tiles(sp, load_w1)

        @block.gpsimd
        def _(pool):
            nc.gpsimd.memset(causal[:], 1.0).then_inc(zeroed, 1)
            nc.gpsimd.memset(ident[:], 0.0).then_inc(zeroed, 1)
            nc.gpsimd.memset(select[:], 0.0).then_inc(zeroed, 1)
            nc.gpsimd.memset(diag[:], 1.0).then_inc(zeroed, 1)
            nc.gpsimd.memset(parity[:], 1.0).then_inc(zeroed, 1)
            nc.gpsimd.memset(before_b[:], 1.0).then_inc(zeroed, 1)
            nc.gpsimd.memset(ln_power[:], -0.5).then_inc(consts, 1)
            nc.gpsimd.memset(ln_eps[:], LN_EPS).then_inc(consts, 1)
            nc.gpsimd.memset(ones_b[:], 1.0).then_inc(consts, 1)
            nc.gpsimd.memset(ones_row[:], 1.0).then_inc(consts, 1)
            pool.wait_ge(zeroed, 6)
            sel = nc.gpsimd.affine_select
            sel(out=causal[:], in_=causal[:], compare_op=ALU.is_ge, fill=0.0, base=0,
                pattern=[[1, P]], channel_multiplier=-1).then_inc(consts, 1)
            sel(out=before_b[:], in_=before_b[:], compare_op=ALU.is_gt, fill=0.0, base=0,
                pattern=[[1, P]], channel_multiplier=-1).then_inc(consts, 1)
            sel(out=ident[:], in_=ident[:], compare_op=ALU.not_equal, fill=1.0, base=0,
                pattern=[[-1, P]], channel_multiplier=1).then_inc(consts, 1)
            for j in range(4):
                v = select[:, HV * j:HV * (j + 1)]
                sel(out=v, in_=v, compare_op=ALU.not_equal, fill=1.0, base=-32 * j,
                    pattern=[[-1, HV]], channel_multiplier=1).then_inc(consts, 1)
            sel(out=diag[:], in_=diag[:], compare_op=ALU.is_ge, fill=0.0, base=0,
                pattern=[[-HD, HALF], [0, HV]], channel_multiplier=1).then_inc(zeroed, 1)
            pool.wait_ge(zeroed, 7)
            sel(out=diag[:], in_=diag[:], compare_op=ALU.is_ge, fill=0.0, base=HD - 1,
                pattern=[[HD, HALF], [0, HV]], channel_multiplier=-1).then_inc(consts, 1)
            for j in range(4):
                v = iota_i[:, j:j + 1]
                nc.gpsimd.iota(v, pattern=[[0, 1]], base=0, channel_multiplier=1).then_inc(zeroed, 1)
            pool.wait_ge(zeroed, 11)
            nc.gpsimd.iota(part1_i[:], pattern=[[0, 1]], base=1, channel_multiplier=1).then_inc(iotas, 1)
            nc.gpsimd.iota(tval_i[:], pattern=[[1, BLOCKS], [BLOCKS, BATCH]], base=0,
                           channel_multiplier=0).then_inc(iotas, 1)
            nc.gpsimd.iota(iota_i[:], pattern=[[1, P]], base=0, channel_multiplier=0).then_inc(iotas, 1)
            pool.wait_ge(vec_consts, 2)

            def kmasks(t, par):
                pool.wait_ge(phi_done, t + 1)
                if not (isinstance(t, int) and t < 2):
                    pool.wait_ge(sc_done, t - 1)
                for e in range(2):
                    nc.gpsimd.tensor_tensor(kmask[:, par, e].rearrange("p c n -> p (c n)"),
                                            phi[:, par, 2:4].rearrange("p c n -> p (c n)"),
                                            parity[:, e:e + 1].broadcast_to([P, KC * P]),
                                            ALU.mult).then_inc(kmask_done, 1)

            def add_state(t, b):
                pool.wait_ge(kv_masked, t + 1)
                pool.wait_ge(nat_done, t + 1)
                nc.gpsimd.tensor_tensor(state[:, b], state[:, b], state_add[:], ALU.add
                                        ).then_inc(state_done, 1)

            def power(t, par):
                pool.wait_ge(mv_done, t + 1)
                nc.gpsimd.tensor_tensor(veps[:, par:par + 1], mv[:, par, 1:2], ln_eps[:], ALU.add
                                        ).then_inc(veps_done, 1)
                pool.wait_ge(veps_done, t + 1)
                nc.gpsimd.tensor_tensor(rstd[:, par:par + 1], veps[:, par:par + 1], ln_power[:], ALU.pow
                                        ).then_inc(rstd_done, 1)

            kmasks(0, 0)

            def group(i, first, last):
                for u in range(4):
                    t = 4 * i + u
                    if not (last and u == 3):
                        kmasks(t + 1, (u + 1) % 2)
                    add_state(t, u)
                    if not (first and u == 0):
                        power(t - 1, (u + 1) % 2)

            groups(pool, group)
            power(CHUNKS - 1, (CHUNKS - 1) % 2)

            for b in range(BATCH):
                pool.wait_ge(x1_out[b], 16 * BLOCKS)

            def gather(j, u, met):
                pool.wait_ge(consts, 12)
                if isinstance(j, int) and j < 4:
                    pool.wait_ge(first_gidx, j + 1)
                else:
                    pool.wait_ge(gidx_done, met)
                    pool.wait_ge(z2_done, met)
                nc.gpsimd.indirect_dma_start(
                    out=xg[:, u % 4], out_offset=None, in_=x1_rows,
                    in_offset=bass.IndirectOffsetOnAxis(ap=gidx[:, u % 4:u % 4 + 1], axis=0),
                    bounds_check=TOKENS - 1, oob_is_err=False).then_inc(xg_in[u % 4], 16)

            for j in range(4):
                gather(j, j, 0)

            def tile_j(j, u):
                pool.wait_ge(mv2_done, j + 1)
                nc.gpsimd.tensor_tensor(veps2[:, u % 2:u % 2 + 1], mv2[:, u % 2, 1:2], ln_eps[:],
                                        ALU.add).then_inc(veps2_done, 1)
                pool.wait_ge(veps2_done, j + 1)
                nc.gpsimd.tensor_tensor(rstd2[:, u % 2:u % 2 + 1], veps2[:, u % 2:u % 2 + 1],
                                        ln_power[:], ALU.pow).then_inc(rstd2_done, 1)
                if not (isinstance(j, int) and j + 4 >= TILES):
                    gather(j + 4, u, j + 1)
                pool.wait_ge(consts, 12)
                pool.wait_ge(yo_done, j + 1)
                pool.wait_ge(sidx_done, j + 1)
                nc.gpsimd.indirect_dma_start(
                    out=out.rearrange("b s d -> (b s) d"),
                    out_offset=bass.IndirectOffsetOnAxis(ap=sidx[:, u % 2:u % 2 + 1], axis=0),
                    in_=yo[:, u % 2], in_offset=None,
                    bounds_check=TOKENS - 1, oob_is_err=False).then_inc(y_out[u % 2], 16)

            tiles(pool, tile_j)
            pool.wait_ge(y_out[0], 16 * ((TILES + 1) // 2))
            pool.wait_ge(y_out[1], 16 * (TILES // 2))

        @block.tensor
        def _(pe):
            mm = nc.tensor.matmul

            def scores_and_qk(t, par, more, b, i):
                pe.wait_ge(kmask_done, 2 * (t + 1))
                if not (isinstance(t, int) and t == 0):
                    pe.wait_ge(av_evac, t)
                    pe.wait_ge(att_done, t)
                    pe.wait_ge(kv_masked, t)
                if not (isinstance(t, int) and t < 2):
                    pe.wait_ge(z_done, t - 1)
                for c in range(KC):
                    for e in range(2):
                        for r in range(4):
                            rows = slice(32 * r, 32 * r + 32)
                            m = mm(bank[r][:, (2 * c + e) * P:(2 * c + e + 1) * P],
                                   kmask[rows, par, e, c, :], phi[rows, par, c, :],
                                   start=True, stop=True)
                        if c == KC - 1 and e == 1:
                            m.then_inc(sc_done, 1)
                        if more and 2 * c + e < 2:
                            project_qk(t + 1, b, i, [2 * c + e])
                if more:
                    project_qk(t + 1, b, i, [2, 3])

            def project_qk(t, b, i, slices):
                if slices[0] == 0:
                    pe.wait_ge(xt_in[b], 16 * (i + 1))
                    if not (isinstance(t, int) and t == 0):
                        pe.wait_ge(er_done, 2 * t)
                for s in slices:
                    for c in range(KC):
                        m = mm(b_qk[:, s * P:(s + 1) * P], wqkv[:, c, s * P:(s + 1) * P], xt[:, b, c],
                               start=(c == 0), stop=(c == KC - 1))
                if slices[-1] == 3:
                    m.then_inc(qk_done, 1)

            def project_v(t, b):
                if not (isinstance(t, int) and t == 0):
                    pe.wait_ge(kn_evac, t)
                for c in range(KC):
                    m = mm(b_vk[:, 0:D], xt[:, b, c], wqkv[:, c, 2 * D:3 * D],
                           start=(c == 0), stop=(c == KC - 1))
                m.then_inc(v_done, 1)

            def k_rows(t, par):
                pe.wait_ge(phi_done, t + 1)
                pe.wait_ge(v_evac, t + 1)
                for c in range(KC):
                    m = nc.tensor.transpose(b_vk[:, c * P:(c + 1) * P], phi[:, par, 2 + c], ident[:])
                m.then_inc(kn_done, 1)

            def own_values(t, par):
                for r in range(4):
                    pe.wait_ge(probs_done, 4 * t + r + 1)
                    if r == 0:
                        pe.wait_ge(v_evac, t + 1)
                    for j in range(4):
                        head = HALF * (j // 2) + 2 * r + j % 2
                        m = mm(b_av[32 * j:32 * j + 32, r * P:(r + 1) * P], vext[:, par, head, :],
                               probs[:, r, j], start=True, stop=True)
                m.then_inc(av_done, 1)

            def chunk_state(t, par):
                pe.wait_ge(kn_evac, t + 1)
                for c in range(KC):
                    m = mm(b_kv[:, c * HALF * HV:(c + 1) * HALF * HV], kn[:, par, c * P:(c + 1) * P],
                           vext[:, par, HALF * c:HALF * (c + 1), 0:HV], start=True, stop=True)
                m.then_inc(kv_done, 1)

            def numerators(t, b, par):
                if not (isinstance(t, int) and t < 4):
                    pe.wait_ge(state_done, t - 3)
                for c in range(KC):
                    mm(b_nat[:, c * HALF * HV:(c + 1) * HALF * HV], phi[:, par, c], state[:, b, c],
                       start=(c == 0), stop=False, skip_group_check=True)
                pe.wait_ge(av_evac, t + 1)
                nat = b_nat[:, 0:HEADS * HV].rearrange("p (c r n) -> p c r n", c=KC, r=4)
                for r in range(4):
                    m = mm(nat[:, :, r], avt[:, r], select[:].rearrange("p (c n) -> p c n", c=KC),
                           start=False, stop=(r == 3), skip_group_check=True)
                m.then_inc(nat_done, 1)

            def att_transpose(t):
                pe.wait_ge(att_done, t + 1)
                if not (isinstance(t, int) and t < 2):
                    pe.wait_ge(x1T_evac, t - 1)
                for c in range(KC):
                    m = nc.tensor.transpose(b_tr[:, c * P:(c + 1) * P], att[:, c * P:(c + 1) * P], ident[:])
                m.then_inc(attT_done, 1)

            def project_out(t):
                pe.wait_ge(attT_evac, t + 1)
                if not (isinstance(t, int) and t == 0):
                    pe.wait_ge(z_done, t)
                for c in range(KC):
                    m = mm(b_op[:, 0:D], attT[:, c], wo[:, c], start=(c == 0), stop=(c == KC - 1))
                m.then_inc(op_done, 1)

            def x1_transpose(t, b):
                pe.wait_ge(x1_done, t + 1)
                if isinstance(t, int) and t == CHUNKS - 1:
                    pe.wait_ge(x1T_evac, t)
                elif isinstance(t, int) and t == CHUNKS - 2:
                    pe.wait_ge(attT_evac, t + 2)
                else:
                    pe.wait_ge(attT_evac, t + 2)
                for c in range(KC):
                    m = nc.tensor.transpose(b_tr[:, c * P:(c + 1) * P], x1[:, b, c * P:(c + 1) * P], ident[:])
                m.then_inc(x1T_done, 1)

            def logits(t):
                pe.wait_ge(x1T_evac, t + 1)
                for c in range(KC):
                    m = mm(b_lg[:, bass.ds(t * E, E)], x1T[:, c], wg[:, c], start=(c == 0), stop=(c == KC - 1))
                m.then_inc(lg_done, 1)

            pe.wait_ge(w_in, 16)
            pe.wait_ge(consts, 12)
            project_qk(0, 0, 0, range(4))
            project_v(0, 0)
            k_rows(0, 0)
            pe.wait_ge(w_in, 64)

            def group(i, first, last):
                for u in range(4):
                    t, par = 4 * i + u, u % 2
                    more = not (last and u == 3)
                    scores_and_qk(t, par, more, (u + 1) % 4, i + (u + 1) // 4)
                    if more:
                        project_v(t + 1, (u + 1) % 4)
                    if not (first and u < 1):
                        att_transpose(t - 1)
                    own_values(t, par)
                    chunk_state(t, par)
                    numerators(t, u, par)
                    if not (first and u < 2):
                        x1_transpose(t - 2, (u + 2) % 4)
                    if not (first and u < 1):
                        project_out(t - 1)
                    if more:
                        k_rows(t + 1, (u + 1) % 2)
                    if not (first and u < 2):
                        logits(t - 2)

            groups(pe, group)
            att_transpose(CHUNKS - 1)
            project_out(CHUNKS - 1)
            x1_transpose(CHUNKS - 2, 2)
            logits(CHUNKS - 2)
            x1_transpose(CHUNKS - 1, 3)
            logits(CHUNKS - 1)

            pe.wait_ge(route, R_ONEHOT)
            mm(bank[0][:, 0:CHUNKS * E], before_b[:], onehot_b[:], start=True, stop=True).then_inc(count_done, 1)
            mm(bank[1][:, 0:CHUNKS * E], ones_b[:], onehot_b[:], start=True, stop=True).then_inc(count_done, 1)
            pe.wait_ge(mov_done, 5)
            for t in range(CHUNKS):
                pe.wait_ge(lo_hot_done, t + 1)
                m = mm(bank[2][:, 0:5 * TILES], lo_hot[:, t], mov[:, t].rearrange("p a n -> p (a n)"),
                       start=(t == 0), stop=(t == CHUNKS - 1))
            m.then_inc(slots_done, 1)

            b_h = [[bank[0], bank[1]], [bank[2], bank[3]]]
            b_y = [bank[4], bank[5]]
            b_xt = [bank[6], bank[7]]

            def rows_transpose(j, u):
                pe.wait_ge(xg_in[u % 4], 16 * (j // 4 + 1) if isinstance(j, int) else 4 * (j - u % 4 + 4))
                if not (isinstance(j, int) and j < 2):
                    pe.wait_ge(xgT_evac, j - 1)
                for c in range(KC):
                    m = nc.tensor.transpose(b_xt[u % 2][:, c * P:(c + 1) * P],
                                            xg[:, u % 4, c * P:(c + 1) * P], ident[:])
                m.then_inc(xgT_done, 1)

            def hidden(j, u):
                pe.wait_ge(w1_in[u % 2], 16 * (j // 2 + 1) if isinstance(j, int) else 8 * (j - u % 2 + 2))
                pe.wait_ge(xgT_evac, j + 1)
                if not (isinstance(j, int) and j < 2):
                    pe.wait_ge(h_act, 4 * (j - 1))
                    pe.wait_ge(h_vec, 4 * (j - 1))
                for g in range(2):
                    for f in range(4):
                        for c in range(KC):
                            at = c * F + (4 * g + f) * P
                            m = mm(b_h[u % 2][g][:, f * P:(f + 1) * P], w1s[:, u % 2, at:at + P],
                                   xgT[:, u % 2, c], start=(c == 0), stop=(c == KC - 1))
                    m.then_inc(h_done, 1)

            def outputs(j, u):
                e = pe.value_load(expert_i[0:1, bass.ds(j, 1)], min_val=0, max_val=E - 1)
                if not (isinstance(j, int) and j < 2):
                    pe.wait_ge(yb_done, j - 1)
                for f in range(FC):
                    if f == 0:
                        pe.wait_ge(h_act, 4 * j + 4)
                    if f == 4:
                        pe.wait_ge(h_vec, 4 * j + 4)
                    m = mm(b_y[u % 2][:, 0:D], hT[:, u % 2, f], w2s[:, bass.ds(e * (FC * D) + f * D, D)],
                           start=(f == 0), stop=(f == FC - 1))
                m.then_inc(y_done, 1)

            pe.wait_ge(w2_in, 16 * E)
            pe.wait_ge(experts_ready, 1)
            rows_transpose(0, 0)
            rows_transpose(1, 1)
            hidden(0, 0)

            def step(j, u):
                if not (isinstance(j, int) and j + 1 >= TILES):
                    hidden(j + 1, u + 1)
                if not (isinstance(j, int) and j + 2 >= TILES):
                    rows_transpose(j + 2, u + 2)
                outputs(j, u)

            tiles(pe, step)

        @block.scalar
        def _(act):
            def exp_relu(t):
                act.wait_ge(qk_done, t + 1)
                if not (isinstance(t, int) and t == 0):
                    act.wait_ge(phi_done, t)
                nc.scalar.activation(expo[:], b_qk[:], ACT.Exp).then_inc(er_done, 1)
                nc.scalar.activation(relu[:], b_qk[:], ACT.Relu).then_inc(er_done, 1)

            def copy_v(t, par):
                act.wait_ge(v_done, t + 1)
                if not (isinstance(t, int) and t < 2):
                    act.wait_ge(kv_done, t - 1)
                nc.scalar.activation(vext[:, par, :, 0:HD], b_vk[:, 0:D].rearrange("p (h n) -> p h n", h=HEADS),
                                     ACT.Copy).then_inc(v_evac, 1)

            def copy_kn(t, par):
                act.wait_ge(kn_done, t + 1)
                if not (isinstance(t, int) and t < 2):
                    act.wait_ge(kv_done, t - 1)
                nc.scalar.activation(kn[:, par], b_vk[:, 0:D], ACT.Copy).then_inc(kn_evac, 1)

            def copy_av(t):
                act.wait_ge(av_done, t + 1)
                if not (isinstance(t, int) and t == 0):
                    act.wait_ge(nat_done, t)
                nc.scalar.activation(avt[:].rearrange("p r n -> p (r n)"), b_av[:], ACT.Copy).then_inc(av_evac, 1)

            def copy_attT(t):
                act.wait_ge(attT_done, t + 1)
                if not (isinstance(t, int) and t == 0):
                    act.wait_ge(op_done, t)
                nc.scalar.activation(attT[:].rearrange("p c n -> p (c n)"), b_tr[:, 0:D], ACT.Copy
                                     ).then_inc(attT_evac, 1)

            def copy_x1T(t):
                act.wait_ge(x1T_done, t + 1)
                if not (isinstance(t, int) and t == 0):
                    act.wait_ge(lg_done, t)
                nc.scalar.activation(x1T[:].rearrange("p c n -> p (c n)"), b_tr[:, 0:D], ACT.Copy
                                     ).then_inc(x1T_evac, 1)

            act.wait_ge(vec_consts, 4)
            exp_relu(0)
            copy_v(0, 0)
            copy_kn(0, 0)

            def group(i, first, last):
                for u in range(4):
                    t = 4 * i + u
                    more = not (last and u == 3)
                    if more:
                        exp_relu(t + 1)
                        copy_v(t + 1, (u + 1) % 2)
                    if not (first and u < 1):
                        copy_attT(t - 1)
                    copy_av(t)
                    if not (first and u < 2):
                        copy_x1T(t - 2)
                    if more:
                        copy_kn(t + 1, (u + 1) % 2)

            groups(act, group)
            copy_attT(CHUNKS - 1)
            copy_x1T(CHUNKS - 2)
            copy_x1T(CHUNKS - 1)

            act.wait_ge(route, R_SHIFTED)
            nc.scalar.activation(ex[:], lg[:], ACT.Exp).then_inc(exp_done, 1)

            def relu_h(j, u):
                act.wait_ge(h_done, 2 * j + 1)
                act.wait_ge(w1_in[u % 2], 16 * (j // 2 + 1) if isinstance(j, int) else 8 * (j - u % 2 + 2))
                if not (isinstance(j, int) and j < 2):
                    act.wait_ge(y_done, j - 1)
                for f in range(4):
                    nc.scalar.activation(hT[:, u % 2, f], [bank[0], bank[2]][u % 2][:, f * P:(f + 1) * P],
                                         ACT.Relu, bias=w1s[:, u % 2, KC * F + f:KC * F + f + 1]
                                         ).then_inc(h_act, 1)

            def copy_rows(j, u):
                act.wait_ge(xgT_done, j + 1)
                if not (isinstance(j, int) and j < 2):
                    act.wait_ge(h_done, 2 * (j - 1))
                nc.scalar.activation(xgT[:, u % 2].rearrange("p c n -> p (c n)"),
                                     [bank[6], bank[7]][u % 2][:, 0:D], ACT.Copy).then_inc(xgT_evac, 1)

            def step(j, u):
                if not (isinstance(j, int) and j + 1 >= TILES):
                    relu_h(j + 1, u + 1)
                if not (isinstance(j, int) and j + 2 >= TILES):
                    copy_rows(j + 2, u + 2)

            copy_rows(0, 0)
            copy_rows(1, 1)
            relu_h(0, 0)
            tiles(act, step)

        @block.vector
        def _(dve):
            V = nc.vector
            V.memset(vext[:], 1.0).then_inc(vec_consts, 1)
            dve.wait_ge(iotas, 3)
            V.tensor_copy(part1[:], part1_i[:]).then_inc(route, 1)
            dve.wait_ge(route, 1)
            V.tensor_scalar(lo_i[:, 0:1], part1_i[:], 1, None, ALU.subtract).then_inc(route, 1)
            dve.wait_ge(route, 2)
            V.tensor_scalar(hi_i[:, 0:1], lo_i[:, 0:1], 4, 1, ALU.logical_shift_right, ALU.bitwise_and
                            ).then_inc(route, 1)
            dve.wait_ge(route, 3)
            dve.wait_ge(zeroed, 11)
            V.tensor_copy(parity[:, 1:2], hi_i[:, 0:1]).then_inc(vec_consts, 1)
            V.tensor_scalar(parity[:, 0:1], hi_i[:, 0:1], -1.0, 1.0, ALU.mult, ALU.add).then_inc(vec_consts, 1)
            V.memset(state[:], 0.0).then_inc(vec_consts, 1)
            V.tensor_copy(iota_p[:], iota_i[:]).then_inc(route, 1)
            V.tensor_copy(iota_b[:], iota_i[:]).then_inc(route, 1)
            V.tensor_copy(tval[:], tval_i[:]).then_inc(route, 1)
            dve.wait_ge(route, 6)
            V.tensor_scalar(rank8[:], iota_p[:, 0:E], -1.0, float(E), ALU.mult, ALU.add).then_inc(route, 1)
            V.tensor_scalar(steps[:], iota_p[:, 0:CHUNKS], float(P), None, ALU.mult).then_inc(route, 1)
            dve.wait_ge(consts, 12)

            def mask_scores(t):
                dve.wait_ge(sc_done, t + 1)
                if not (isinstance(t, int) and t == 0):
                    dve.wait_ge(av_done, t)
                for r in range(4):
                    V.tensor_tensor(probs[:, r], bank[r][:].rearrange("p (j n) -> p j n", j=4),
                                    causal[:].rearrange("p (a n) -> p a n", a=1).broadcast_to([P, 4, P]),
                                    ALU.mult).then_inc(probs_done, 1)

            def phi_map(t, par):
                dve.wait_ge(er_done, 2 * t + 2)
                if not (isinstance(t, int) and t < 2):
                    dve.wait_ge(nat_done, t - 1)
                    dve.wait_ge(kn_done, t - 1)
                    dve.wait_ge(kmask_done, 2 * (t - 1))
                V.scalar_tensor_tensor(phi[:, par].rearrange("p s n -> p (s n)"), expo[:], 1.0, relu[:],
                                       ALU.min, ALU.add).then_inc(phi_done, 1)

            def mask_state(t):
                dve.wait_ge(kv_done, t + 1)
                if not (isinstance(t, int) and t == 0):
                    dve.wait_ge(state_done, t)
                V.tensor_tensor(state_add[:].rearrange("p c (h n) -> p c h n", h=HALF),
                                b_kv[:, 0:HEADS * HV].rearrange("p (c h n) -> p c h n", c=KC, h=HALF),
                                diag[:].rearrange("p (a h) n -> p a h n", a=1).broadcast_to([P, KC, HALF, HV]),
                                ALU.mult).then_inc(kv_masked, 1)

            def divide(t):
                dve.wait_ge(nat_done, t + 1)
                nat = b_nat[:, 0:HEADS * HV].rearrange("p (h n) -> p h n", h=HEADS)
                V.tensor_scalar(den[:], nat[:, :, HD], DEN_EPS, None, ALU.add).then_inc(den_done, 1)
                dve.wait_ge(den_done, t + 1)
                V.reciprocal(rden[:], den[:]).then_inc(rden_done, 1)
                dve.wait_ge(rden_done, t + 1)
                if not (isinstance(t, int) and t == 0):
                    dve.wait_ge(attT_done, t)
                V.tensor_tensor(att[:].rearrange("p (h n) -> p h n", h=HEADS), nat[:, :, 0:HD],
                                rden[:].rearrange("p (h a) -> p h a", a=1).broadcast_to([P, HEADS, HD]),
                                ALU.mult).then_inc(att_done, 1)

            def residual(t, b, i, par):
                dve.wait_ge(op_done, t + 1)
                dve.wait_ge(xn_in[b], 16 * (i + 1))
                V.tensor_tensor(z[:, par], b_op[:, 0:D], xn[:, b], ALU.add).then_inc(z_done, 1)
                dve.wait_ge(z_done, t + 1)
                V.bn_stats(stats[:], z[:, par]).then_inc(stats_done, 1)
                dve.wait_ge(consts, 12)
                dve.wait_ge(stats_done, t + 1)
                V.bn_aggr(mv[:, par], stats[:]).then_inc(mv_done, 1)

            def normalise(t, b, i, par):
                dve.wait_ge(rstd_done, t + 1)
                dve.wait_ge(mv_done, t + 1)
                if not (isinstance(t, int) and t < 4):
                    dve.wait_ge(x1_out[b], 16 * i)
                    dve.wait_ge(x1T_done, t - 2)
                V.tensor_scalar(x1[:, b], z[:, par], mv[:, par, 0:1], rstd[:, par:par + 1],
                                ALU.subtract, ALU.mult).then_inc(x1_done, 1)

            phi_map(0, 0)

            def group(i, first, last):
                for u in range(4):
                    t, par = 4 * i + u, u % 2
                    mask_scores(t)
                    if not (last and u == 3):
                        phi_map(t + 1, (u + 1) % 2)
                    if not (first and u < 2):
                        normalise(t - 2, (u + 2) % 4, i + (u + 2) // 4 - 1, par)
                    mask_state(t)
                    divide(t)
                    if not (first and u < 1):
                        residual(t - 1, (u + 3) % 4, i + (u + 3) // 4 - 1, (u + 1) % 2)

            groups(dve, group)
            normalise(CHUNKS - 2, 2, BLOCKS - 1, 0)
            residual(CHUNKS - 1, 3, BLOCKS - 1, 1)
            normalise(CHUNKS - 1, 3, BLOCKS - 1, 1)

            step_no = [R_CONSTS]

            def then(ins):
                step_no[0] += 1
                ins.then_inc(route, 1)
                dve.wait_ge(route, step_no[0])

            def over_e(ap):
                return ap.rearrange("p (t a) -> p t a", a=1).broadcast_to([P, CHUNKS, E])

            def over_t(ap):
                return ap.rearrange("p (a e) -> p a e", a=1).broadcast_to([P, CHUNKS, E])

            def e_over_t(ap):
                return ap.rearrange("p (e a) -> p e a", a=1).broadcast_to([P, E, CHUNKS])

            dve.wait_ge(lg_done, CHUNKS)
            dve.wait_ge(w_in, 64)
            then(V.tensor_tensor(lg[:], b_lg[:, 0:CHUNKS * E].rearrange("p (t e) -> p t e", t=CHUNKS),
                                 over_t(bg[:]), ALU.add))
            then(V.tensor_reduce(lmax[:], lg[:], AX_X, ALU.max))
            then(V.tensor_tensor(lg[:], lg[:], over_e(lmax[:]), ALU.subtract))
            assert step_no[0] == R_SHIFTED
            then(V.scalar_tensor_tensor(hit[:], lg[:], 0.0, over_t(rank8[:]), ALU.is_ge, ALU.mult))
            then(V.tensor_reduce(first[:], hit[:], AX_X, ALU.max))
            then(V.tensor_tensor(onehot[:], hit[:], over_e(first[:]), ALU.is_equal))
            then(V.tensor_copy(onehot_b[:], onehot[:].rearrange("p t e -> p (t e)")))
            assert step_no[0] == R_ONEHOT
            dve.wait_ge(exp_done, 1)
            then(V.tensor_reduce(esum[:], ex[:], AX_X, ALU.add))
            then(V.reciprocal(top_p[:], esum[:]))
            then(V.tensor_copy(p_part[:, 0], top_p[:]))
            then(V.tensor_tensor(p_rest[:, 0], top_p[:], p_part[:, 0], ALU.subtract))
            then(V.tensor_copy(p_part[:, 1], p_rest[:, 0]))
            then(V.tensor_tensor(p_rest[:, 1], p_rest[:, 0], p_part[:, 1], ALU.subtract))
            then(V.tensor_copy(p_part[:, 2], p_rest[:, 1]))
            dve.wait_ge(count_done, 2)
            then(V.tensor_copy(total[:], bank[1][:, 0:CHUNKS * E].rearrange("p (t e) -> p e t", t=CHUNKS)))
            then(V.tensor_tensor_scan(cum[:].rearrange("p e t -> p (e t)"), ones_row[:],
                                      total[:].rearrange("p e t -> p (e t)"), 0.0, ALU.mult, ALU.add))
            then(V.tensor_copy(estart[:, 1:E], cum[:, 0:E - 1, CHUNKS - 1]))
            then(V.memset(estart[:, 0:1], 0.0))
            then(V.tensor_tensor(count[:], cum[:, :, CHUNKS - 1], estart[:], ALU.subtract))
            then(V.tensor_tensor(over[:], e_over_t(count[:]),
                                 steps[:].rearrange("p (a t) -> p a t", a=1).broadcast_to([P, E, CHUNKS]),
                                 ALU.is_gt))
            then(V.tensor_reduce(ntile[:], over[:], AX_X, ALU.add))
            then(V.tensor_tensor_scan(tend[:], ones_row[:, 0:E], ntile[:], 0.0, ALU.mult, ALU.add))
            then(V.tensor_tensor(shift[:], tend[:], ntile[:], ALU.subtract))
            then(V.scalar_tensor_tensor(shift[:], shift[:], float(P), estart[:], ALU.mult, ALU.subtract))
            then(V.tensor_tensor(base[:], cum[:], total[:], ALU.subtract))
            then(V.tensor_tensor(base[:], base[:], e_over_t(shift[:]), ALU.add))
            then(V.tensor_tensor(pick[:], bank[0][:, 0:CHUNKS * E].rearrange("p (t e) -> p t e", t=CHUNKS),
                                 base[:].rearrange("p e t -> p t e"), ALU.add))
            then(V.tensor_tensor(pick[:], pick[:], onehot[:], ALU.mult))
            then(V.tensor_reduce(slot[:], pick[:], AX_X, ALU.add))
            then(V.tensor_copy(slot_i[:], slot[:]))
            then(V.tensor_scalar(hi_i[:], slot_i[:], 7, None, ALU.logical_shift_right))
            then(V.tensor_scalar(lo_i[:], slot_i[:], P - 1, None, ALU.bitwise_and))
            then(V.tensor_copy(hi[:], hi_i[:]))
            then(V.tensor_copy(lo[:], lo_i[:]))
            then(V.tensor_tensor(hi_hot[:],
                                 iota_p[:, 0:TILES].rearrange("p (a n) -> p a n", a=1).broadcast_to([P, CHUNKS, TILES]),
                                 hi[:].rearrange("p (t a) -> p t a", a=1).broadcast_to([P, CHUNKS, TILES]),
                                 ALU.is_equal))
            V.tensor_scalar(mov[:, :, 0], hi_hot[:], part1[:], None, ALU.mult).then_inc(mov_done, 1)
            for a, factor in enumerate([tval[:], p_part[:, 0], p_part[:, 1], p_part[:, 2]]):
                V.tensor_tensor(mov[:, :, 1 + a], hi_hot[:],
                                factor.rearrange("p (t a) -> p t a", a=1).broadcast_to([P, CHUNKS, TILES]),
                                ALU.mult).then_inc(mov_done, 1)
            for t in range(CHUNKS):
                V.tensor_scalar(lo_hot[:, t], iota_b[:], lo[:, t:t + 1], None, ALU.is_equal
                                ).then_inc(lo_hot_done, 1)
            then(V.tensor_tensor(ended[:], iota_p[:, 0:TILES].rearrange("p (n a) -> p n a", a=1).broadcast_to([P, TILES, E]),
                                 tend[:].rearrange("p (a e) -> p a e", a=1).broadcast_to([P, TILES, E]), ALU.is_ge))
            then(V.tensor_reduce(expert_f[:], ended[:], AX_X, ALU.add))
            then(V.tensor_scalar(expert_f[:], expert_f[:], float(E - 1), None, ALU.min))
            V.tensor_copy(expert_i[:], expert_f[:]).then_inc(experts_ready, 1)
            dve.wait_ge(slots_done, 1)
            then(V.tensor_copy(slot_sb[:].rearrange("p a n -> p (a n)"), bank[2][:, 0:5 * TILES]))
            then(V.scalar_tensor_tensor(tok1[:], slot_sb[:, 1], float(P), slot_sb[:, 0], ALU.mult, ALU.add))
            then(V.tensor_scalar(gather_f[:], tok1[:], -1.0, 0.0, ALU.add, ALU.max))
            then(V.tensor_copy(gather_i[:], gather_f[:]))
            then(V.tensor_scalar(scatter_f[:], tok1[:], 0.0, float(2 * TOKENS), ALU.is_equal, ALU.mult))
            then(V.scalar_tensor_tensor(scatter_f[:], tok1[:], -1.0, scatter_f[:], ALU.add, ALU.add))
            then(V.tensor_copy(scatter_i[:], scatter_f[:]))
            then(V.tensor_tensor(slot_p2[:], slot_sb[:, 3], slot_sb[:, 4], ALU.add))
            then(V.tensor_tensor(slot_p[:], slot_sb[:, 2], slot_p2[:], ALU.add))

            def next_index(j, u):
                if not (isinstance(j, int) and j < 4):
                    dve.wait_ge(xg_in[u % 4], 16 * (j // 4) if isinstance(j, int) else 4 * (j - u % 4))
                first = isinstance(j, int) and j < 4
                V.tensor_copy(gidx[:, u % 4:u % 4 + 1], gather_i[:, bass.ds(j, 1)]
                              ).then_inc(first_gidx if first else gidx_done, 1)

            def relu_h(j, u):
                dve.wait_ge(h_done, 2 * j + 2)
                dve.wait_ge(w1_in[u % 2], 16 * (j // 2 + 1) if isinstance(j, int) else 8 * (j - u % 2 + 2))
                if not (isinstance(j, int) and j < 2):
                    dve.wait_ge(y_done, j - 1)
                for f in range(4, FC):
                    V.tensor_scalar(hT[:, u % 2, f], [bank[1], bank[3]][u % 2][:, (f - 4) * P:(f - 3) * P],
                                    w1s[:, u % 2, KC * F + f:KC * F + f + 1], 0.0, ALU.add, ALU.max
                                    ).then_inc(h_vec, 1)

            def finish(j, u):
                dve.wait_ge(y_done, j + 1)
                dve.wait_ge(b2_in[u % 4], 16 * (j // 4 + 1) if isinstance(j, int) else 4 * (j - u % 4 + 4))
                if not (isinstance(j, int) and j < 1):
                    dve.wait_ge(z2_done, j)
                V.tensor_tensor(yb[:], [bank[4], bank[5]][u % 2][:, 0:D], b2s[:, u % 4], ALU.add
                                ).then_inc(yb_done, 1)
                dve.wait_ge(yb_done, j + 1)
                dve.wait_ge(xg_in[u % 4], 16 * (j // 4 + 1) if isinstance(j, int) else 4 * (j - u % 4 + 4))
                V.scalar_tensor_tensor(z2[:, u % 2], yb[:], slot_p[:, bass.ds(j, 1)], xg[:, u % 4],
                                       ALU.mult, ALU.add).then_inc(z2_done, 1)
                dve.wait_ge(z2_done, j + 1)
                V.bn_stats(stats2[:], z2[:, u % 2]).then_inc(stats2_done, 1)
                dve.wait_ge(consts, 12)
                dve.wait_ge(stats2_done, j + 1)
                V.bn_aggr(mv2[:, u % 2], stats2[:]).then_inc(mv2_done, 1)

            def normalise2(j, u):
                dve.wait_ge(rstd2_done, j + 1)
                dve.wait_ge(mv2_done, j + 1)
                if not (isinstance(j, int) and j < 2):
                    dve.wait_ge(y_out[u % 2], 16 * (j // 2) if isinstance(j, int) else 8 * (j - u % 2))
                V.tensor_copy(sidx[:, u % 2:u % 2 + 1], scatter_i[:, bass.ds(j, 1)]).then_inc(sidx_done, 1)
                V.tensor_scalar(yo[:, u % 2], z2[:, u % 2], mv2[:, u % 2, 0:1], rstd2[:, u % 2:u % 2 + 1],
                                ALU.subtract, ALU.mult).then_inc(yo_done, 1)

            next_index(0, 0)
            next_index(1, 1)
            next_index(2, 2)
            next_index(3, 3)
            relu_h(0, 0)

            def step(j, u):
                if not (isinstance(j, int) and j + 1 >= TILES):
                    relu_h(j + 1, u + 1)
                if not (isinstance(j, int) and j + 4 >= TILES):
                    next_index(j + 4, u)
                finish(j, u)
                normalise2(j, u)

            tiles(dve, step)


R_CONSTS = 8
R_SHIFTED = R_CONSTS + 3
R_ONEHOT = R_SHIFTED + 4


def kernel(**inputs):
    import numpy as np
    import concourse.bacc as bacc
    from concourse.bass_utils import run_bass_kernel_spmd as run

    x = np.ascontiguousarray(inputs["L0_attn_x"])
    w1 = np.asarray(inputs["L0_ffn_W1"])
    b1 = np.asarray(inputs["L0_ffn_b1"])
    arrays = {
        "x": x,
        "xT": np.ascontiguousarray(x.reshape(BATCH, BLOCKS, P, KC, P).transpose(1, 0, 4, 3, 2)),
        "w_qkv": np.ascontiguousarray(inputs["L0_attn_W_qkv"]),
        "w_out": np.ascontiguousarray(inputs["L0_attn_W_out"]),
        "w_gate": np.ascontiguousarray(inputs["L0_ffn_w_gate"]),
        "b_gate": np.ascontiguousarray(inputs["L0_ffn_b_gate"]),
        "w1b": np.ascontiguousarray(np.concatenate([
            w1.reshape(E, KC, P, F).transpose(0, 2, 1, 3).reshape(E, P, KC * F),
            b1.reshape(E, FC, P).transpose(0, 2, 1)], axis=2)),
        "w2": np.ascontiguousarray(inputs["L0_ffn_W2"]),
        "b2": np.ascontiguousarray(inputs["L0_ffn_b2"]),
    }
    nc = bacc.Bacc("TRN2", target_bir_lowering=False, num_devices=1)
    args = [nc.dram_tensor(n, a.shape, mybir.dt.from_np(a.dtype), kind="ExternalInput").ap()
            for n, a in arrays.items()]
    out = nc.dram_tensor("out", (BATCH, SEQ, D), F32, kind="ExternalOutput").ap()
    attention_moe(nc, *args, out)
    r = run(nc, [arrays], core_ids=[0])
    return r.results[0]["out"]
```

```python
from contextlib import ExitStack

import concourse.bass as bass
from concourse import mybir

ALU = mybir.AluOpType
ACT = mybir.ActivationFunctionType
F32 = mybir.dt.float32
F32R = mybir.dt.float32r
BF16 = mybir.dt.bfloat16
I32 = mybir.dt.int32
U32 = mybir.dt.uint32
AX_X = mybir.AxisListType.X

P = 128
BATCH, SEQ, D = 4, 1024, 256
HEADS, HD = 16, 16
HV = HD + 1
E, F = 8, 1024
TOKENS = BATCH * SEQ
CHUNKS = TOKENS // P
BLOCKS = SEQ // P
KC = D // P
FC = F // P
TILES = CHUNKS + E - 1
HALF = HEADS // KC
PRODUCTS = [(0, 0), (0, 1), (1, 0)]
ROW_TILES = [(0, 2), (1, 3)]
W2_PIECE = FC * D // BATCH
assert E == BLOCKS
LN_EPS = 1e-5
DEN_EPS = 1e-6
W1_ROW = KC * F + FC


def attention_moe(nc, x, xT, w_qkv, w_out, w_gate, b_gate, w1b, w2, b2, out):
    with ExitStack() as ctx:
        def sb(name, shape, dt=F32):
            return ctx.enter_context(nc.sbuf_tensor(name, shape, dt))

        attention = ExitStack()

        def sa(name, shape, dt=F32):
            return attention.enter_context(nc.sbuf_tensor(name, shape, dt))

        def sem(name):
            return ctx.enter_context(nc.semaphore(name))

        x1_rows = nc.dram_tensor("x1_rows", (TOKENS, D + 1), F32, kind="Internal").ap()

        bg = sb("bg", [P, E])
        w2_high = sb("w2_high", [P, E * FC * D], F32R)
        w2_low = sb("w2_low", [P, E * FC * D], F32R)
        ident = sb("ident", [P, P])
        iota_i = sb("iota_i", [P, P], I32)
        ln_power = sb("ln_power", [P, 1])
        ln_eps = sb("ln_eps", [P, 1])
        lg = sb("lg", [P, 4, E])
        rank8 = sb("rank8", [P, E])
        before_b = sb("before_b", [P, P], BF16)
        ones_b = sb("ones_b", [P, P], BF16)
        hi_i = sb("hi_i", [P, CHUNKS], I32)
        lo_i = sb("lo_i", [P, CHUNKS], I32)
        iota_p = sb("iota_p", [P, P])
        iota_b = sb("iota_b", [P, P], BF16)
        part1_i = sb("part1_i", [P, 1], I32)
        part1 = sb("part1", [P, 1])
        tval_i = sb("tval_i", [P, CHUNKS], I32)
        tval = sb("tval", [P, CHUNKS])
        lmax = sb("lmax", [P, 4])
        ex = sb("ex", [P, 4, E])
        esum = sb("esum", [P, 4])
        top_p = sb("top_p", [P, CHUNKS])
        hit = sb("hit", [P, 4, E])
        first_hit = sb("first_hit", [P, 4])
        onehot = sb("onehot", [P, CHUNKS, E])
        onehot_b = sb("onehot_b", [P, CHUNKS * E], BF16)
        prefix_b = sb("prefix_b", [P, (CHUNKS + 1) * E], BF16)
        ones_e = sb("ones_e", [P, E])
        xt = sa("xt", [P, BATCH, KC, P])
        xn = sa("xn", [P, BATCH, D])
        expo = sa("expo", [P, 4 * P])
        relu = sa("relu", [P, 4 * P])
        phi = sa("phi", [P, 2, 4, P])
        q_part = sa("q_part", [P, 2, KC, 2, P], F32R)
        k_part = sa("k_part", [P, 2, KC, P], F32R)
        vext = sa("vext", [P, 2, HEADS, 32])
        kn = sa("kn", [P, 2, D])
        probs = sa("probs", [P, 4, 4, P])
        avt = sa("avt", [P, 4, P])
        state = sa("state", [P, BATCH, KC, HALF * HV])
        state_add = sa("state_add", [P, KC, HALF * HV])
        den = sa("den", [P, HEADS])
        rden = sa("rden", [P, HEADS])
        att = sa("att", [P, D])
        attT = sa("attT", [P, 2, KC, P], F32R)
        x_part = sa("x_part", [P, 2, KC, P], F32R)
        z = sa("z", [P, 2, D])
        stats = sa("stats", [P, 6])
        mv = sa("mv", [P, 2, 2])
        veps = sa("veps", [P, 2])
        rstd = sa("rstd", [P, 2])
        x1 = sa("x1", [P, BATCH, D])
        x1T = sa("x1T", [P, KC, P])
        wqk = sa("wqk", [P, KC, 2 * D])
        wv_part = sa("wv_part", [P, 2, KC, D], F32R)
        wo_part = sa("wo_part", [P, 2, KC, D], F32R)
        wg = sa("wg", [P, KC, E])
        causal = sa("causal", [P, P])
        select = sa("select", [P, 4 * HV])
        diag = sa("diag", [P, HALF, HV])
        parity = sa("parity", [P, 2])
        w2_half = sa("w2_half", [P, FC * D // 2])
        attention.close()
        pick = sb("pick", [P, CHUNKS, E])
        count_i = sb("count_i", [P, E], I32)
        tiles_i = sb("tiles_i", [P, E], I32)
        tstart = sb("tstart", [P, E])
        ntile = sb("ntile", [P, E])
        tend = sb("tend", [P, E])
        slot = sb("slot", [P, CHUNKS])
        slot_i = sb("slot_i", [P, CHUNKS], I32)
        hi = sb("hi", [P, CHUNKS])
        lo = sb("lo", [P, CHUNKS])
        lo_hot = sb("lo_hot", [P, CHUNKS, P], BF16)
        hi_hot = sb("hi_hot", [P, CHUNKS, TILES], BF16)
        mov = sb("mov", [P, CHUNKS, 2, TILES], BF16)
        slot_sb = sb("slot_sb", [P, 2, TILES])
        tok1 = sb("tok1", [P, TILES])
        gather_f = sb("gather_f", [P, TILES])
        scatter_f = sb("scatter_f", [P, TILES])
        gather_i = sb("gather_i", [P, TILES], U32)
        scatter_i = sb("scatter_i", [P, TILES], U32)
        ended = sb("ended", [P, TILES, E])
        expert_f = sb("expert_f", [P, TILES])
        expert_i = sb("expert_i", [P, TILES], I32)
        w1s = sb("w1s", [P, 2, W1_ROW])
        b2s = sb("b2s", [P, 4, D])
        gidx = sb("gidx", [P, 4], U32)
        sidx = sb("sidx", [P, 2], U32)
        xg = sb("xg", [P, 4, D + 1])
        xgT = sb("xgT", [P, 2, KC, P])
        hT_high = sb("hT_high", [P, 2, FC, P], F32R)
        hT_low = sb("hT_low", [P, 2, FC, P], F32R)
        hT = sb("hT", [P, FC, P])
        z2 = sb("z2", [P, 2, D])
        stats2 = sb("stats2", [P, 6])
        mv2 = sb("mv2", [P, 2, 2])
        veps2 = sb("veps2", [P, 2])
        rstd2 = sb("rstd2", [P, 2])
        yo = sb("yo", [P, 2, D])

        bank = [ctx.enter_context(nc.psum_tensor(f"bank{i}", [P, 512], F32)) for i in range(8)]
        b_av, b_nat, b_kv, b_op = bank[0], bank[1], bank[2], bank[3]
        b_qk, b_vk, b_tr, b_lg = bank[4], bank[5], bank[6], bank[7]

        raw = probs[:].rearrange("p r j n -> p (r j n)").rearrange("p (w c n) -> p w c n", w=4, c=KC)

        w_in = sem("w_in")
        w2_in = sem("w2_in")
        wvo_in = sem("wvo_in")
        xt_in = [sem(f"xt_in{b}") for b in range(BATCH)]
        xn_in = [sem(f"xn_in{b}") for b in range(BATCH)]
        x1_out = [sem(f"x1_out{b}") for b in range(BATCH)]
        zeroed = sem("zeroed")
        consts = sem("consts")
        iotas = sem("iotas")
        vec_consts = sem("vec_consts")
        qk_done = sem("qk_done")
        v_done = sem("v_done")
        er_done = sem("er_done")
        v_evac = sem("v_evac")
        phi_done = sem("phi_done")
        high_done = sem("high_done")
        q_low_done = sem("q_low_done")
        k_low_done = sem("k_low_done")
        kn_done = sem("kn_done")
        kn_evac = sem("kn_evac")
        sc_done = sem("sc_done")
        probs_done = sem("probs_done")
        av_done = sem("av_done")
        av_evac = sem("av_evac")
        nat_done = sem("nat_done")
        den_done = sem("den_done")
        rden_done = sem("rden_done")
        att_done = sem("att_done")
        kv_done = sem("kv_done")
        kv_masked = sem("kv_masked")
        state_done = sem("state_done")
        attT_done = sem("attT_done")
        attT_evac = sem("attT_evac")
        attT_low = sem("attT_low")
        w_high = sem("w_high")
        w_low = sem("w_low")
        x_high = sem("x_high")
        x_low = sem("x_low")
        op_done = sem("op_done")
        z_done = sem("z_done")
        stats_done = sem("stats_done")
        mv_done = sem("mv_done")
        veps_done = sem("veps_done")
        rstd_done = sem("rstd_done")
        x1_done = sem("x1_done")
        x1T_done = sem("x1T_done")
        x1T_evac = sem("x1T_evac")
        lg_done = sem("lg_done")
        route = sem("route")
        choice = sem("choice")
        exp_done = sem("exp_done")
        p_out = sem("p_out")
        lo_ready = sem("lo_ready")
        lo_hot_pool = sem("lo_hot_pool")
        count_done = sem("count_done")
        lo_hot_done = sem("lo_hot_done")
        mov_done = sem("mov_done")
        slots_done = sem("slots_done")
        experts_ready = sem("experts_ready")
        idx_ready = sem("idx_ready")
        w1_in = [sem(f"w1_in{b}") for b in range(2)]
        b2_in = [sem(f"b2_in{b}") for b in range(4)]
        xg_in = [sem(f"xg_in{b}") for b in range(4)]
        y_out = [sem(f"y_out{b}") for b in range(2)]
        first_gidx = sem("first_gidx")
        gidx_done = sem("gidx_done")
        sidx_done = sem("sidx_done")
        xgT_done = sem("xgT_done")
        xgT_evac = sem("xgT_evac")
        h_done = sem("h_done")
        w2_high_done = sem("w2_high_done")
        w2_low_done = sem("w2_low_done")
        h_high_done = sem("h_high_done")
        h_low_vec = sem("h_low_vec")
        h_low_pool = sem("h_low_pool")
        h_act = sem("h_act")
        h_vec = sem("h_vec")
        y_done = sem("y_done")
        yb_done = sem("yb_done")
        z2_done = sem("z2_done")
        stats2_done = sem("stats2_done")
        mv2_done = sem("mv2_done")
        veps2_done = sem("veps2_done")
        rstd2_done = sem("rstd2_done")
        yo_done = sem("yo_done")

        block = ctx.enter_context(nc.Block())

        def groups(eng, body):
            body(0, True, False)
            with eng.Fori(1, BLOCKS - 1) as i:
                body(i, False, False)
            body(BLOCKS - 1, False, True)

        def tiles(eng, body):
            for j in range(4):
                body(j, j)
            with eng.Fori(1, TILES // 4 - 1) as k:
                for u in range(4):
                    body(4 * k + u, u)
            for j in range((TILES // 4 - 1) * 4, TILES):
                body(j, j % 4)

        @block.sync
        def _(sp):
            w_rows = w_qkv.rearrange("(c p) n -> p c n", p=P)
            sp.dma_start(wqk[:], w_rows[:, :, 0:2 * D]).then_inc(w_in, 16)

            def load(t, i, b):
                sp.dma_start(xt[:, b], xT[bass.ds(i, 1), b].rearrange("a p c n -> (a p) c n")
                             ).then_inc(xt_in[b], 16)
                sp.dma_start(xn[:, b], x[b, bass.ds(i * P, P), :]).then_inc(xn_in[b], 16)

            for b in range(BATCH):
                load(b, 0, b)
                if b == 0:
                    sp.dma_start(raw[:, 0], w_rows[:, :, 2 * D:3 * D]).then_inc(wvo_in, 16)
                    sp.dma_start(raw[:, 1], w_out.rearrange("(c p) n -> p c n", p=P)).then_inc(wvo_in, 16)
                    sp.dma_start(wg[:], w_gate.rearrange("(c p) n -> p c n", p=P)).then_inc(w_in, 16)
                    sp.dma_start(bg[:], b_gate.rearrange("(a e) -> a e", a=1).broadcast_to([P, E])
                                 ).then_inc(w_in, 16)

            def store_x1(t, i, b):
                sp.wait_ge(x1_done, t + 1)
                sp.dma_start(x1_rows[bass.ds(b * SEQ + i * P, P), 0:D], x1[:, b]
                             ).then_inc(x1_out[b], 16)

            with sp.Fori(1, BLOCKS) as i:
                for b in range(BATCH):
                    t = 4 * i + b
                    sp.wait_ge(qk_done, t - 3)
                    sp.wait_ge(x_low, t - 3)
                    sp.wait_ge(z_done, t - 3)
                    load(t, i, b)
                    store_x1(t - 4, i - 1, b)
            for b in range(BATCH):
                store_x1(4 * (BLOCKS - 1) + b, BLOCKS - 1, b)

            sp.wait_ge(experts_ready, 1)

            def load_w1(j, u):
                if not (isinstance(j, int) and j < 2):
                    sp.wait_ge(h_act, 4 * (j - 1))
                    sp.wait_ge(h_vec, 4 * (j - 1))
                e = sp.value_load(expert_i[0:1, bass.ds(j, 1)], min_val=0, max_val=E - 1)
                sp.dma_start(w1s[:, u % 2], w1b[bass.ds(e, 1)].rearrange("a p n -> (a p) n")
                             ).then_inc(w1_in[u % 2], 16)
                if not (isinstance(j, int) and j < 4):
                    sp.wait_ge(yb_done, j - 3)
                sp.dma_start(b2s[:, u % 4], b2[bass.ds(e, 1), :].broadcast_to([P, D])
                             ).then_inc(b2_in[u % 4], 16)

            tiles(sp, load_w1)

        @block.gpsimd
        def _(pool):
            nc.gpsimd.memset(causal[:], 1.0).then_inc(zeroed, 1)
            nc.gpsimd.memset(ident[:], 0.0).then_inc(zeroed, 1)
            nc.gpsimd.memset(select[:], 0.0).then_inc(zeroed, 1)
            nc.gpsimd.memset(diag[:], 1.0).then_inc(zeroed, 1)
            nc.gpsimd.memset(parity[:], 1.0).then_inc(zeroed, 1)
            nc.gpsimd.memset(before_b[:], 1.0).then_inc(zeroed, 1)
            nc.gpsimd.memset(ln_power[:], -0.5).then_inc(consts, 1)
            nc.gpsimd.memset(ln_eps[:], LN_EPS).then_inc(consts, 1)
            nc.gpsimd.memset(ones_b[:], 1.0).then_inc(consts, 1)
            nc.gpsimd.memset(ones_e[:], 1.0).then_inc(consts, 1)
            pool.wait_ge(zeroed, 6)
            sel = nc.gpsimd.affine_select
            sel(out=causal[:], in_=causal[:], compare_op=ALU.is_ge, fill=0.0, base=0,
                pattern=[[1, P]], channel_multiplier=-1).then_inc(consts, 1)
            sel(out=before_b[:], in_=before_b[:], compare_op=ALU.is_gt, fill=0.0, base=0,
                pattern=[[1, P]], channel_multiplier=-1).then_inc(consts, 1)
            sel(out=ident[:], in_=ident[:], compare_op=ALU.not_equal, fill=1.0, base=0,
                pattern=[[-1, P]], channel_multiplier=1).then_inc(consts, 1)
            for j in range(4):
                v = select[:, HV * j:HV * (j + 1)]
                sel(out=v, in_=v, compare_op=ALU.not_equal, fill=1.0, base=-32 * j,
                    pattern=[[-1, HV]], channel_multiplier=1).then_inc(consts, 1)
            sel(out=diag[:], in_=diag[:], compare_op=ALU.is_ge, fill=0.0, base=0,
                pattern=[[-HD, HALF], [0, HV]], channel_multiplier=1).then_inc(zeroed, 1)
            pool.wait_ge(zeroed, 7)
            sel(out=diag[:], in_=diag[:], compare_op=ALU.is_ge, fill=0.0, base=HD - 1,
                pattern=[[HD, HALF], [0, HV]], channel_multiplier=-1).then_inc(consts, 1)
            for j in range(4):
                v = iota_i[:, j:j + 1]
                nc.gpsimd.iota(v, pattern=[[0, 1]], base=0, channel_multiplier=1).then_inc(zeroed, 1)
            pool.wait_ge(zeroed, 11)
            nc.gpsimd.iota(part1_i[:], pattern=[[0, 1]], base=1, channel_multiplier=1).then_inc(iotas, 1)
            nc.gpsimd.iota(tval_i[:], pattern=[[1, BLOCKS], [BLOCKS, BATCH]], base=0,
                           channel_multiplier=0).then_inc(iotas, 1)
            nc.gpsimd.iota(iota_i[:], pattern=[[1, P]], base=0, channel_multiplier=0).then_inc(iotas, 1)
            pool.wait_ge(vec_consts, 2)

            def split_x(t, b):
                pool.wait_ge(x_high, t + 1)
                nc.gpsimd.tensor_tensor(x_part[:, 1].rearrange("p c n -> p (c n)"),
                                        xt[:, b].rearrange("p c n -> p (c n)"),
                                        x_part[:, 0].rearrange("p c n -> p (c n)").bitcast(F32),
                                        ALU.subtract).then_inc(x_low, 1)

            def k_low(t, par):
                pool.wait_ge(high_done, 3 * t + 1)
                nc.gpsimd.tensor_tensor(k_part[:, 1].rearrange("p c n -> p (c n)"),
                                        phi[:, par, 2:4].rearrange("p c n -> p (c n)"),
                                        k_part[:, 0].rearrange("p c n -> p (c n)").bitcast(F32),
                                        ALU.subtract).then_inc(k_low_done, 1)

            def add_state(t, b):
                pool.wait_ge(kv_masked, t + 1)
                pool.wait_ge(nat_done, t + 1)
                nc.gpsimd.tensor_tensor(state[:, b], state[:, b], state_add[:], ALU.add
                                        ).then_inc(state_done, 1)

            def power(t, par):
                pool.wait_ge(mv_done, t + 1)
                nc.gpsimd.tensor_tensor(veps[:, par:par + 1], mv[:, par, 1:2], ln_eps[:], ALU.add
                                        ).then_inc(veps_done, 1)
                pool.wait_ge(veps_done, t + 1)
                nc.gpsimd.tensor_tensor(rstd[:, par:par + 1], veps[:, par:par + 1], ln_power[:], ALU.pow
                                        ).then_inc(rstd_done, 1)

            def split_w2(e, u):
                pool.wait_ge(w2_high_done, 4 * e + u + 1)
                piece = bass.ds((4 * e + u) * W2_PIECE, W2_PIECE)
                nc.gpsimd.tensor_tensor(w2_low[:, piece], w2_half[:, u % 2 * W2_PIECE:(u % 2 + 1) * W2_PIECE],
                                        w2_high[:, piece].bitcast(F32), ALU.subtract).then_inc(w2_low_done, 1)

            split_x(0, 0)
            split_x(1, 1)
            k_low(0, 0)

            def group(i, first, last):
                for u in range(4):
                    t = 4 * i + u
                    for piece in [[2, 3], [], [0, 1], []][u]:
                        if not (first and u == 0):
                            split_w2(i - 1 if u == 0 else i, piece)
                    if not (last and u == 3):
                        k_low(t + 1, (u + 1) % 2)
                    add_state(t, u)
                    if not (first and u == 0):
                        power(t - 1, (u + 1) % 2)
                    if not (last and u >= 2):
                        split_x(t + 2, (u + 2) % 4)

            groups(pool, group)
            power(CHUNKS - 1, (CHUNKS - 1) % 2)
            split_w2(E - 1, 2)
            split_w2(E - 1, 3)

            pool.wait_ge(lo_ready, 1)
            for t in range(LO_HOT_POOL, CHUNKS):
                nc.gpsimd.tensor_scalar(lo_hot[:, t], iota_p[:], lo[:, t:t + 1], None, ALU.is_equal
                                        ).then_inc(lo_hot_pool, 1)

            for b in range(BATCH):
                pool.wait_ge(x1_out[b], 16 * BLOCKS)
            pool.wait_ge(p_out, 16 * BLOCKS)

            def gather(j, u, met):
                pool.wait_ge(consts, 12)
                if isinstance(j, int) and j < 4:
                    pool.wait_ge(first_gidx, j + 1)
                else:
                    pool.wait_ge(gidx_done, met)
                    pool.wait_ge(z2_done, met)
                nc.gpsimd.indirect_dma_start(
                    out=xg[:, u % 4], out_offset=None, in_=x1_rows,
                    in_offset=bass.IndirectOffsetOnAxis(ap=gidx[:, u % 4:u % 4 + 1], axis=0),
                    bounds_check=TOKENS - 1, oob_is_err=False).then_inc(xg_in[u % 4], 16)

            for j in range(4):
                gather(j, j, 0)

            def split_h(j, u):
                pool.wait_ge(h_high_done, 2 * j + 2)
                nc.gpsimd.tensor_tensor(hT_low[:, u % 2, 4:FC].rearrange("p f n -> p (f n)"),
                                        hT[:, 4:FC].rearrange("p f n -> p (f n)"),
                                        hT_high[:, u % 2, 4:FC].rearrange("p f n -> p (f n)").bitcast(F32),
                                        ALU.subtract).then_inc(h_low_pool, 1)

            split_h(0, 0)

            def tile_j(j, u):
                if not (isinstance(j, int) and j + 1 >= TILES):
                    split_h(j + 1, u + 1)
                pool.wait_ge(mv2_done, j + 1)
                nc.gpsimd.tensor_tensor(veps2[:, u % 2:u % 2 + 1], mv2[:, u % 2, 1:2], ln_eps[:],
                                        ALU.add).then_inc(veps2_done, 1)
                pool.wait_ge(veps2_done, j + 1)
                nc.gpsimd.tensor_tensor(rstd2[:, u % 2:u % 2 + 1], veps2[:, u % 2:u % 2 + 1],
                                        ln_power[:], ALU.pow).then_inc(rstd2_done, 1)
                if not (isinstance(j, int) and j + 4 >= TILES):
                    gather(j + 4, u, j + 1)
                pool.wait_ge(consts, 12)
                pool.wait_ge(yo_done, j + 1)
                pool.wait_ge(sidx_done, j + 1)
                nc.gpsimd.indirect_dma_start(
                    out=out.rearrange("b s d -> (b s) d"),
                    out_offset=bass.IndirectOffsetOnAxis(ap=sidx[:, u % 2:u % 2 + 1], axis=0),
                    in_=yo[:, u % 2], in_offset=None,
                    bounds_check=TOKENS - 1, oob_is_err=False).then_inc(y_out[u % 2], 16)

            tiles(pool, tile_j)
            pool.wait_ge(y_out[0], 16 * ((TILES + 1) // 2))
            pool.wait_ge(y_out[1], 16 * (TILES // 2))

        @block.tensor
        def _(pe):
            mm = nc.tensor.matmul

            def scores_and_qk(t, par, more, b, i):
                pe.wait_ge(q_low_done, 2 * (t + 1))
                pe.wait_ge(k_low_done, t + 1)
                for n, pair in enumerate(ROW_TILES):
                    if not (isinstance(t, int) and t == 0):
                        pe.wait_ge([av_evac, att_done][n], t)
                        if n == 0:
                            pe.wait_ge(kv_masked, t)
                    if n == 1 and not (isinstance(t, int) and t < 2):
                        pe.wait_ge(z_done, t - 1)
                    for c in range(KC):
                        for kp, qp in PRODUCTS:
                            for r in pair:
                                rows = slice(32 * r, 32 * r + 32)
                                m = mm(bank[r][:, 2 * c * P:2 * (c + 1) * P], k_part[rows, kp, c, :],
                                       q_part[rows, qp, c].rearrange("p e n -> p (e n)"),
                                       start=(kp + qp == 0), stop=(kp == 1))
                    m.then_inc(sc_done, 1)
                    if more:
                        project_qk(t + 1, b, i, [n])
                if more:
                    project_qk(t + 1, b, i, [2, 3])

            def project_qk(t, b, i, slices):
                if slices[0] == 0:
                    pe.wait_ge(xt_in[b], 16 * (i + 1))
                    if not (isinstance(t, int) and t == 0):
                        pe.wait_ge(er_done, 2 * t)
                for s in slices:
                    for c in range(KC):
                        m = mm(b_qk[:, s * P:(s + 1) * P], wqk[:, c, s * P:(s + 1) * P], xt[:, b, c],
                               start=(c == 0), stop=(c == KC - 1))
                if slices[-1] == 3:
                    m.then_inc(qk_done, 1)

            def project_v(t, b):
                if not (isinstance(t, int) and t == 0):
                    pe.wait_ge(kn_evac, t)
                pe.wait_ge(x_low, t + 1)
                for c in range(KC):
                    for xp, wp in PRODUCTS:
                        m = mm(b_vk[:, 0:D], x_part[:, xp, c], wv_part[:, wp, c],
                               start=(c == 0 and xp + wp == 0), stop=(c == KC - 1 and xp == 1))
                m.then_inc(v_done, 1)

            def k_rows(t, par):
                pe.wait_ge(phi_done, t + 1)
                pe.wait_ge(v_evac, t + 1)
                for c in range(KC):
                    m = nc.tensor.transpose(b_vk[:, c * P:(c + 1) * P], phi[:, par, 2 + c], ident[:])
                m.then_inc(kn_done, 1)

            def own_values(t, par):
                for n, r in enumerate(ROW_TILES[0] + ROW_TILES[1]):
                    pe.wait_ge(probs_done, 4 * t + n + 1)
                    if n == 0:
                        pe.wait_ge(v_evac, t + 1)
                    for j in range(4):
                        head = HALF * (j // 2) + 2 * r + j % 2
                        m = mm(b_av[32 * j:32 * j + 32, r * P:(r + 1) * P], vext[:, par, head, :],
                               probs[:, r, j], start=True, stop=True)
                m.then_inc(av_done, 1)

            def chunk_state(t, par):
                pe.wait_ge(kn_evac, t + 1)
                for c in range(KC):
                    m = mm(b_kv[:, c * HALF * HV:(c + 1) * HALF * HV], kn[:, par, c * P:(c + 1) * P],
                           vext[:, par, HALF * c:HALF * (c + 1), 0:HV], start=True, stop=True)
                m.then_inc(kv_done, 1)

            def numerators(t, b, par):
                if not (isinstance(t, int) and t < 4):
                    pe.wait_ge(state_done, t - 3)
                for c in range(KC):
                    mm(b_nat[:, c * HALF * HV:(c + 1) * HALF * HV], phi[:, par, c], state[:, b, c],
                       start=(c == 0), stop=False, skip_group_check=True)
                pe.wait_ge(av_evac, t + 1)
                nat = b_nat[:, 0:HEADS * HV].rearrange("p (c r n) -> p c r n", c=KC, r=4)
                for r in range(4):
                    m = mm(nat[:, :, r], avt[:, r], select[:].rearrange("p (c n) -> p c n", c=KC),
                           start=False, stop=(r == 3), skip_group_check=True)
                m.then_inc(nat_done, 1)

            def att_transpose(t):
                pe.wait_ge(att_done, t + 1)
                if not (isinstance(t, int) and t < 2):
                    pe.wait_ge(x1T_evac, t - 1)
                for c in range(KC):
                    m = nc.tensor.transpose(b_tr[:, c * P:(c + 1) * P], att[:, c * P:(c + 1) * P], ident[:])
                m.then_inc(attT_done, 1)

            def project_out(t):
                pe.wait_ge(attT_low, t + 1)
                if not (isinstance(t, int) and t == 0):
                    pe.wait_ge(z_done, t)
                for c in range(KC):
                    for ap, wp in PRODUCTS:
                        m = mm(b_op[:, 0:D], attT[:, ap, c], wo_part[:, wp, c],
                               start=(c == 0 and ap + wp == 0), stop=(c == KC - 1 and ap == 1))
                m.then_inc(op_done, 1)

            def x1_transpose(t, b):
                pe.wait_ge(x1_done, t + 1)
                if isinstance(t, int) and t == CHUNKS - 1:
                    pe.wait_ge(x1T_evac, t)
                elif isinstance(t, int) and t == CHUNKS - 2:
                    pe.wait_ge(attT_low, t + 2)
                else:
                    pe.wait_ge(attT_low, t + 2)
                for c in range(KC):
                    m = nc.tensor.transpose(b_tr[:, c * P:(c + 1) * P], x1[:, b, c * P:(c + 1) * P], ident[:])
                m.then_inc(x1T_done, 1)

            def logits(t, read=None):
                pe.wait_ge(x1T_evac, t + 1)
                if read is not None:
                    pe.wait_ge(choice, C_STEPS * (read - 1) + 1)
                for c in range(KC):
                    m = mm(b_lg[:, bass.ds(t * E, E)], x1T[:, c], wg[:, c], start=(c == 0), stop=(c == KC - 1))
                m.then_inc(lg_done, 1)

            def keep_clock(n):
                for _ in range(n):
                    mm(b_lg[:, 256:384], ident[:], ident[:], start=True, stop=True)

            pe.wait_ge(consts, 12)
            keep_clock(WARM[0])
            pe.wait_ge(w_in, 16)
            project_qk(0, 0, 0, range(4))
            keep_clock(WARM[1])
            pe.wait_ge(w_low, 2)
            project_v(0, 0)
            k_rows(0, 0)
            keep_clock(WARM[2])
            pe.wait_ge(w_in, 48)

            def group(i, first, last):
                for u in range(4):
                    t, par = 4 * i + u, u % 2
                    more = not (last and u == 3)
                    scores_and_qk(t, par, more, (u + 1) % 4, i + (u + 1) // 4)
                    if more:
                        project_v(t + 1, (u + 1) % 4)
                    if not (first and u < 1):
                        att_transpose(t - 1)
                    own_values(t, par)
                    chunk_state(t, par)
                    numerators(t, u, par)
                    if not (first and u < 2):
                        x1_transpose(t - 2, (u + 2) % 4)
                    if not (first and u < 1):
                        project_out(t - 1)
                    if more:
                        k_rows(t + 1, (u + 1) % 2)
                    if not (first and u < 2):
                        logits(t - 2, None if first or u < 2 else i)

            groups(pe, group)
            att_transpose(CHUNKS - 1)
            project_out(CHUNKS - 1)
            x1_transpose(CHUNKS - 2, 2)
            logits(CHUNKS - 2)
            x1_transpose(CHUNKS - 1, 3)
            logits(CHUNKS - 1)

            pe.wait_ge(choice, C_STEPS * (BLOCKS - 1) + C_COUNTED)
            mm(bank[1][:, 0:E], ones_b[:], prefix_b[:, CHUNKS * E:], start=True, stop=True).then_inc(count_done, 1)
            mm(bank[0][:, 0:CHUNKS * E], before_b[:], onehot_b[:], start=True, stop=False)
            mm(bank[0][:, 0:CHUNKS * E], ones_b[:], prefix_b[:, 0:CHUNKS * E], start=False, stop=True).then_inc(count_done, 1)
            pe.wait_ge(mov_done, 2)
            for t in range(CHUNKS):
                if t < LO_HOT_POOL:
                    pe.wait_ge(lo_hot_done, t + 1)
                else:
                    pe.wait_ge(lo_hot_pool, t - LO_HOT_POOL + 1)
                m = mm(bank[2][:, 0:2 * TILES], lo_hot[:, t], mov[:, t].rearrange("p a n -> p (a n)"),
                       start=(t == 0), stop=(t == CHUNKS - 1))
            m.then_inc(slots_done, 1)
            keep_clock(WARM[3])

            b_h = [[bank[0], bank[1]], [bank[2], bank[3]]]
            b_y = [bank[4], bank[5]]
            b_xt = [bank[6], bank[7]]

            def rows_transpose(j, u):
                pe.wait_ge(xg_in[u % 4], 16 * (j // 4 + 1) if isinstance(j, int) else 4 * (j - u % 4 + 4))
                if not (isinstance(j, int) and j < 2):
                    pe.wait_ge(xgT_evac, j - 1)
                for c in range(KC):
                    m = nc.tensor.transpose(b_xt[u % 2][:, c * P:(c + 1) * P],
                                            xg[:, u % 4, c * P:(c + 1) * P], ident[:])
                m.then_inc(xgT_done, 1)

            def hidden(j, u):
                pe.wait_ge(w1_in[u % 2], 16 * (j // 2 + 1) if isinstance(j, int) else 8 * (j - u % 2 + 2))
                pe.wait_ge(xgT_evac, j + 1)
                if not (isinstance(j, int) and j < 2):
                    pe.wait_ge(h_act, 4 * (j - 1))
                    pe.wait_ge(h_vec, 4 * (j - 1))
                for g in range(2):
                    for f in range(4):
                        for c in range(KC):
                            at = c * F + (4 * g + f) * P
                            m = mm(b_h[u % 2][g][:, f * P:(f + 1) * P], w1s[:, u % 2, at:at + P],
                                   xgT[:, u % 2, c], start=(c == 0), stop=(c == KC - 1))
                    m.then_inc(h_done, 1)

            def outputs(j, u):
                e = pe.value_load(expert_i[0:1, bass.ds(j, 1)], min_val=0, max_val=E - 1)
                if not (isinstance(j, int) and j < 2):
                    pe.wait_ge(yb_done, j - 1)
                for f in range(FC):
                    if f == 0:
                        pe.wait_ge(h_low_vec, j + 1)
                    if f == 4:
                        pe.wait_ge(h_low_pool, j + 1)
                    w = bass.ds(e * (FC * D) + f * D, D)
                    for hp, wp in PRODUCTS:
                        m = mm(b_y[u % 2][:, 0:D], [hT_high, hT_low][hp][:, u % 2, f], [w2_high, w2_low][wp][:, w],
                               start=(f == 0 and hp + wp == 0), stop=(f == FC - 1 and hp == 1))
                m.then_inc(y_done, 1)

            pe.wait_ge(w2_low_done, CHUNKS)
            pe.wait_ge(experts_ready, 1)
            rows_transpose(0, 0)
            rows_transpose(1, 1)
            hidden(0, 0)

            def step(j, u):
                if not (isinstance(j, int) and j + 1 >= TILES):
                    hidden(j + 1, u + 1)
                if not (isinstance(j, int) and j + 2 >= TILES):
                    rows_transpose(j + 2, u + 2)
                outputs(j, u)

            tiles(pe, step)

        @block.scalar
        def _(act):
            def exp_relu(t):
                act.wait_ge(qk_done, t + 1)
                if not (isinstance(t, int) and t == 0):
                    act.wait_ge(phi_done, t)
                nc.scalar.activation(expo[:], b_qk[:], ACT.Exp).then_inc(er_done, 1)
                nc.scalar.activation(relu[:], b_qk[:], ACT.Relu).then_inc(er_done, 1)

            def copy_v(t, par):
                act.wait_ge(v_done, t + 1)
                if not (isinstance(t, int) and t < 2):
                    act.wait_ge(kv_done, t - 1)
                nc.scalar.activation(vext[:, par, :, 0:HD], b_vk[:, 0:D].rearrange("p (h n) -> p h n", h=HEADS),
                                     ACT.Copy).then_inc(v_evac, 1)

            def copy_kn(t, par):
                act.wait_ge(kn_done, t + 1)
                if not (isinstance(t, int) and t < 2):
                    act.wait_ge(kv_done, t - 1)
                nc.scalar.activation(kn[:, par], b_vk[:, 0:D], ACT.Copy).then_inc(kn_evac, 1)

            def split_x(t, b, i):
                act.wait_ge(xt_in[b], 16 * (i + 1))
                if not (isinstance(t, int) and t == 0):
                    act.wait_ge(v_done, t)
                nc.scalar.activation(x_part[:, 0], xt[:, b], ACT.Copy).then_inc(x_high, 1)

            def split_phi(t, par):
                act.wait_ge(phi_done, t + 1)
                if not (isinstance(t, int) and t == 0):
                    act.wait_ge(sc_done, 2 * t)
                nc.scalar.activation(k_part[:, 0], phi[:, par, 2:4], ACT.Copy).then_inc(high_done, 1)
                for e in range(2):
                    nc.scalar.activation(q_part[:, 0, :, e], phi[:, par, 0:2], ACT.Relu, scale=parity[:, e:e + 1]
                                         ).then_inc(high_done, 1)

            def copy_av(t):
                act.wait_ge(av_done, t + 1)
                if not (isinstance(t, int) and t == 0):
                    act.wait_ge(nat_done, t)
                nc.scalar.activation(avt[:].rearrange("p r n -> p (r n)"), b_av[:], ACT.Copy).then_inc(av_evac, 1)

            def copy_attT(t):
                act.wait_ge(attT_done, t + 1)
                if not (isinstance(t, int) and t == 0):
                    act.wait_ge(op_done, t)
                nc.scalar.activation(attT[:, 0].rearrange("p c n -> p (c n)"), b_tr[:, 0:D], ACT.Copy
                                     ).then_inc(attT_evac, 1)

            def copy_x1T(t):
                act.wait_ge(x1T_done, t + 1)
                if not (isinstance(t, int) and t == 0):
                    act.wait_ge(lg_done, t)
                nc.scalar.activation(x1T[:].rearrange("p c n -> p (c n)"), b_tr[:, 0:D], ACT.Copy
                                     ).then_inc(x1T_evac, 1)

            def store_p(i):
                act.wait_ge(choice, C_STEPS * (i + 1))
                nc.scalar.dma_start(x1_rows.rearrange("(b i p) c -> i p b c", b=BATCH, i=BLOCKS)[bass.ds(i, 1), :, :, D:D + 1]
                             .rearrange("i p b c -> p (i b) c"),
                             top_p[:, bass.ds(i * BATCH, BATCH)].rearrange("p (b c) -> p b c", c=1),
                             allow_slow_non_contiguous=True).then_inc(p_out, 16)

            def load_w2(e, half):
                if not (isinstance(e, int) and e == 0 and half == 0):
                    act.wait_ge(w2_low_done, 4 * e + 2 * half)
                nc.scalar.dma_start(w2_half[:].rearrange("p (c n) -> p c n", c=FC // 2),
                                    w2[bass.ds(e, 1)].rearrange("a (h c p) n -> p (a h) c n", p=P, h=2)[:, half]
                                    ).then_inc(w2_in, 16)

            def split_w2(e, u):
                act.wait_ge(w2_in, 32 * e + 16 * (u // 2 + 1))
                piece = bass.ds((4 * e + u) * W2_PIECE, W2_PIECE)
                nc.scalar.activation(w2_high[:, piece], w2_half[:, u % 2 * W2_PIECE:(u % 2 + 1) * W2_PIECE], ACT.Copy
                                     ).then_inc(w2_high_done, 1)

            def exp_logits(g):
                act.wait_ge(choice, C_STEPS * g + C_SHIFTED)
                nc.scalar.activation(ex[:].rearrange("p t e -> p (t e)"),
                                     lg[:].rearrange("p t e -> p (t e)"), ACT.Exp
                                     ).then_inc(exp_done, 1)

            act.wait_ge(vec_consts, 4)
            act.wait_ge(wvo_in, 32)
            for n, part in enumerate([wv_part, wo_part]):
                nc.scalar.activation(part[:, 0], raw[:, n], ACT.Copy).then_inc(w_high, 1)
            split_x(0, 0, 0)
            exp_relu(0)
            copy_v(0, 0)
            split_x(1, 1, 0)
            split_phi(0, 0)
            copy_kn(0, 0)

            def group(i, first, last):
                for u in range(4):
                    t = 4 * i + u
                    more = not (last and u == 3)
                    if more:
                        exp_relu(t + 1)
                        copy_v(t + 1, (u + 1) % 2)
                    if not (first and u < 1):
                        copy_attT(t - 1)
                    copy_av(t)
                    if more:
                        split_phi(t + 1, (u + 1) % 2)
                    if not (first and u < 2):
                        copy_x1T(t - 2)
                    if more:
                        copy_kn(t + 1, (u + 1) % 2)
                    if not (last and u >= 2):
                        split_x(t + 2, (u + 2) % 4, i + (u + 2) // 4)
                    if u % 2 == 0:
                        load_w2(i, u // 2)
                    for piece in [[], [0, 1], [], [2, 3]][u]:
                        split_w2(i, piece)
                    if u == 2 and not first:
                        exp_logits(i - 1)
                    if u == 3 and not first:
                        store_p(i - 1)

            groups(act, group)
            copy_attT(CHUNKS - 1)
            copy_x1T(CHUNKS - 2)
            copy_x1T(CHUNKS - 1)
            exp_logits(BLOCKS - 1)
            store_p(BLOCKS - 1)

            def relu_h(j, u):
                act.wait_ge(h_done, 2 * j + 1)
                act.wait_ge(w1_in[u % 2], 16 * (j // 2 + 1) if isinstance(j, int) else 8 * (j - u % 2 + 2))
                if not (isinstance(j, int) and j < 1):
                    act.wait_ge(h_low_vec, j)
                for f in range(4):
                    nc.scalar.activation(hT[:, f], [bank[0], bank[2]][u % 2][:, f * P:(f + 1) * P],
                                         ACT.Relu, bias=w1s[:, u % 2, KC * F + f:KC * F + f + 1]
                                         ).then_inc(h_act, 1)

            def copy_rows(j, u):
                act.wait_ge(xgT_done, j + 1)
                if not (isinstance(j, int) and j < 2):
                    act.wait_ge(h_done, 2 * (j - 1))
                nc.scalar.activation(xgT[:, u % 2].rearrange("p c n -> p (c n)"),
                                     [bank[6], bank[7]][u % 2][:, 0:D], ACT.Copy).then_inc(xgT_evac, 1)

            def split_h(j, u):
                for g, relued in enumerate([h_act, h_vec]):
                    act.wait_ge(relued, 4 * j + 4)
                    if g == 0 and not (isinstance(j, int) and j < 2):
                        act.wait_ge(y_done, j - 1)
                    nc.scalar.activation(hT_high[:, u % 2, 4 * g:4 * g + 4].rearrange("p f n -> p (f n)"),
                                         hT[:, 4 * g:4 * g + 4].rearrange("p f n -> p (f n)"),
                                         ACT.Copy).then_inc(h_high_done, 1)

            def step(j, u):
                if not (isinstance(j, int) and j + 1 >= TILES):
                    relu_h(j + 1, u + 1)
                if not (isinstance(j, int) and j + 2 >= TILES):
                    copy_rows(j + 2, u + 2)
                if not (isinstance(j, int) and j + 1 >= TILES):
                    split_h(j + 1, u + 1)

            copy_rows(0, 0)
            copy_rows(1, 1)
            relu_h(0, 0)
            split_h(0, 0)
            tiles(act, step)

        @block.vector
        def _(dve):
            V = nc.vector
            V.memset(vext[:], 1.0).then_inc(vec_consts, 1)
            dve.wait_ge(iotas, 3)
            V.tensor_copy(part1[:], part1_i[:]).then_inc(route, 1)
            dve.wait_ge(route, 1)
            V.tensor_scalar(lo_i[:, 0:1], part1_i[:], 1, None, ALU.subtract).then_inc(route, 1)
            dve.wait_ge(route, 2)
            V.tensor_scalar(hi_i[:, 0:1], lo_i[:, 0:1], 4, 1, ALU.logical_shift_right, ALU.bitwise_and
                            ).then_inc(route, 1)
            dve.wait_ge(route, 3)
            dve.wait_ge(zeroed, 11)
            V.tensor_copy(parity[:, 1:2], hi_i[:, 0:1]).then_inc(vec_consts, 1)
            V.tensor_scalar(parity[:, 0:1], hi_i[:, 0:1], -1.0, 1.0, ALU.mult, ALU.add).then_inc(vec_consts, 1)
            V.memset(state[:], 0.0).then_inc(vec_consts, 1)
            V.tensor_copy(iota_p[:], iota_i[:]).then_inc(route, 1)
            V.tensor_copy(iota_b[:], iota_i[:]).then_inc(route, 1)
            V.tensor_copy(tval[:], tval_i[:]).then_inc(route, 1)
            dve.wait_ge(route, 6)
            V.tensor_scalar(rank8[:], iota_p[:, 0:E], -1.0, float(E), ALU.mult, ALU.add).then_inc(route, 1)
            V.memset(prefix_b[:, 0:E], 0.0).then_inc(route, 1)
            dve.wait_ge(consts, 12)

            def mask_scores(t):
                dve.wait_ge(sc_done, 2 * t + 1)
                if not (isinstance(t, int) and t == 0):
                    dve.wait_ge(av_done, t)
                for n, r in enumerate(ROW_TILES[0] + ROW_TILES[1]):
                    if n == 2:
                        dve.wait_ge(sc_done, 2 * t + 2)
                    V.tensor_tensor(probs[:, r], bank[r][:].rearrange("p (j n) -> p j n", j=4),
                                    causal[:].rearrange("p (a n) -> p a n", a=1).broadcast_to([P, 4, P]),
                                    ALU.mult).then_inc(probs_done, 1)

            def phi_map(t, par):
                dve.wait_ge(er_done, 2 * t + 2)
                if not (isinstance(t, int) and t < 2):
                    dve.wait_ge(nat_done, t - 1)
                    dve.wait_ge(kn_done, t - 1)
                    dve.wait_ge(high_done, 3 * (t - 1))
                    dve.wait_ge(k_low_done, t - 1)
                V.scalar_tensor_tensor(phi[:, par].rearrange("p s n -> p (s n)"), expo[:], 1.0, relu[:],
                                       ALU.min, ALU.add).then_inc(phi_done, 1)

            def q_low(t, par):
                for e in range(2):
                    dve.wait_ge(high_done, 3 * t + 2 + e)
                    V.scalar_tensor_tensor(q_part[:, 1, :, e], phi[:, par, 0:2], parity[:, e:e + 1],
                                           q_part[:, 0, :, e].bitcast(F32), ALU.mult, ALU.subtract
                                           ).then_inc(q_low_done, 1)

            def mask_state(t):
                dve.wait_ge(kv_done, t + 1)
                if not (isinstance(t, int) and t == 0):
                    dve.wait_ge(state_done, t)
                V.tensor_tensor(state_add[:].rearrange("p c (h n) -> p c h n", h=HALF),
                                b_kv[:, 0:HEADS * HV].rearrange("p (c h n) -> p c h n", c=KC, h=HALF),
                                diag[:].rearrange("p (a h) n -> p a h n", a=1).broadcast_to([P, KC, HALF, HV]),
                                ALU.mult).then_inc(kv_masked, 1)

            def divide(t):
                dve.wait_ge(nat_done, t + 1)
                nat = b_nat[:, 0:HEADS * HV].rearrange("p (h n) -> p h n", h=HEADS)
                V.tensor_scalar(den[:], nat[:, :, HD], DEN_EPS, None, ALU.add).then_inc(den_done, 1)
                dve.wait_ge(den_done, t + 1)
                V.reciprocal(rden[:], den[:]).then_inc(rden_done, 1)
                dve.wait_ge(rden_done, t + 1)
                if not (isinstance(t, int) and t == 0):
                    dve.wait_ge(attT_done, t)
                V.tensor_tensor(att[:].rearrange("p (h n) -> p h n", h=HEADS), nat[:, :, 0:HD],
                                rden[:].rearrange("p (h a) -> p h a", a=1).broadcast_to([P, HEADS, HD]),
                                ALU.mult).then_inc(att_done, 1)

            def attT_split(t):
                dve.wait_ge(attT_evac, t + 1)
                V.tensor_tensor(attT[:, 1].rearrange("p c n -> p (c n)"), b_tr[:, 0:D],
                                attT[:, 0].rearrange("p c n -> p (c n)").bitcast(F32), ALU.subtract
                                ).then_inc(attT_low, 1)

            def residual(t, b, i, par):
                dve.wait_ge(op_done, t + 1)
                dve.wait_ge(xn_in[b], 16 * (i + 1))
                V.tensor_tensor(z[:, par], b_op[:, 0:D], xn[:, b], ALU.add).then_inc(z_done, 1)
                dve.wait_ge(z_done, t + 1)
                V.bn_stats(stats[:], z[:, par]).then_inc(stats_done, 1)
                dve.wait_ge(consts, 12)
                dve.wait_ge(stats_done, t + 1)
                V.bn_aggr(mv[:, par], stats[:]).then_inc(mv_done, 1)

            def normalise(t, b, i, par):
                dve.wait_ge(rstd_done, t + 1)
                dve.wait_ge(mv_done, t + 1)
                if not (isinstance(t, int) and t < 4):
                    dve.wait_ge(x1_out[b], 16 * i)
                    dve.wait_ge(x1T_done, t - 2)
                V.tensor_scalar(x1[:, b], z[:, par], mv[:, par, 0:1], rstd[:, par:par + 1],
                                ALU.subtract, ALU.mult).then_inc(x1_done, 1)

            def over_e4(ap):
                return ap.rearrange("p (t a) -> p t a", a=1).broadcast_to([P, 4, E])

            def over_t4(ap):
                return ap.rearrange("p (a e) -> p a e", a=1).broadcast_to([P, 4, E])

            def choose(g, n):
                tt = bass.ds(4 * g, 4)
                if n > 1:
                    dve.wait_ge(choice, C_STEPS * g + n - 1)
                if n == 1:
                    dve.wait_ge(lg_done, 4 * g + 4)
                    V.tensor_tensor(lg[:], b_lg[:, bass.ds(4 * E * g, 4 * E)]
                                    .rearrange("p (t e) -> p t e", t=4), over_t4(bg[:]), ALU.add
                                    ).then_inc(choice, 1)
                elif n == 2:
                    V.tensor_reduce(lmax[:], lg[:], AX_X, ALU.max).then_inc(choice, 1)
                elif n == 3:
                    V.tensor_tensor(lg[:], lg[:], over_e4(lmax[:]), ALU.subtract).then_inc(choice, 1)
                elif n == 4:
                    V.scalar_tensor_tensor(hit[:], lg[:], 0.0, over_t4(rank8[:]), ALU.is_ge, ALU.mult
                                           ).then_inc(choice, 1)
                elif n == 5:
                    V.tensor_reduce(first_hit[:], hit[:], AX_X, ALU.max).then_inc(choice, 1)
                elif n == 6:
                    V.tensor_tensor(onehot[:, tt], hit[:], over_e4(first_hit[:]), ALU.is_equal
                                    ).then_inc(choice, 1)
                elif n == 7:
                    V.tensor_copy(onehot_b[:, bass.ds(4 * E * g, 4 * E)],
                                  onehot[:, tt].rearrange("p t e -> p (t e)")).then_inc(choice, 1)
                elif n < 8 + 4:
                    at = E * (4 * g + n - 8)
                    V.tensor_tensor(prefix_b[:, bass.ds(at + E, E)], prefix_b[:, bass.ds(at, E)],
                                    onehot_b[:, bass.ds(at, E)], ALU.add).then_inc(choice, 1)
                elif n == 8 + 4:
                    dve.wait_ge(exp_done, g + 1)
                    V.tensor_reduce(esum[:], ex[:], AX_X, ALU.add).then_inc(choice, 1)
                elif n == 9 + 4:
                    V.reciprocal(top_p[:, tt], esum[:]).then_inc(choice, 1)

            for n, part in enumerate([wv_part, wo_part]):
                dve.wait_ge(w_high, n + 1)
                V.tensor_tensor(part[:, 1], raw[:, n], part[:, 0].bitcast(F32), ALU.subtract).then_inc(w_low, 1)
            phi_map(0, 0)
            q_low(0, 0)

            def group(i, first, last):
                for u in range(4):
                    t, par = 4 * i + u, u % 2

                    def choose_after(n):
                        if u >= 2 and not first:
                            for m in [[[1], [2], [3], [4], [5, 6]], [[7], [8], [9, 10], [11, 12], [13]]][u - 2][n - 1]:
                                choose(i - 1, m)

                    choose_after(1)
                    mask_scores(t)
                    choose_after(2)
                    if not (last and u == 3):
                        phi_map(t + 1, (u + 1) % 2)
                    if not (first and u < 1):
                        attT_split(t - 1)
                    choose_after(3)
                    if not (first and u < 2):
                        normalise(t - 2, (u + 2) % 4, i + (u + 2) // 4 - 1, par)
                    choose_after(4)
                    mask_state(t)
                    if not (last and u == 3):
                        q_low(t + 1, (u + 1) % 2)
                    choose_after(5)
                    divide(t)
                    if not (first and u < 1):
                        residual(t - 1, (u + 3) % 4, i + (u + 3) // 4 - 1, (u + 1) % 2)

            groups(dve, group)
            normalise(CHUNKS - 2, 2, BLOCKS - 1, 0)
            attT_split(CHUNKS - 1)
            residual(CHUNKS - 1, 3, BLOCKS - 1, 1)
            normalise(CHUNKS - 1, 3, BLOCKS - 1, 1)

            step_no = [R_CONSTS]

            def then(ins):
                step_no[0] += 1
                ins.then_inc(route, 1)
                dve.wait_ge(route, step_no[0])

            for n in range(1, C_STEPS + 1):
                choose(BLOCKS - 1, n)
            dve.wait_ge(count_done, 1)
            then(V.tensor_scalar(count_i[:], bank[1][:, 0:E], float(P - 1), None, ALU.add))
            then(V.tensor_scalar(tiles_i[:], count_i[:], 7, None, ALU.logical_shift_right))
            then(V.tensor_copy(ntile[:], tiles_i[:]))
            then(V.tensor_tensor_scan(tend[:], ones_e[:], ntile[:], 0.0, ALU.mult, ALU.add))
            then(V.tensor_tensor(tstart[:], tend[:], ntile[:], ALU.subtract))
            dve.wait_ge(count_done, 2)
            then(V.scalar_tensor_tensor(pick[:], tstart[:].rearrange("p (a e) -> p a e", a=1).broadcast_to([P, CHUNKS, E]),
                                        float(P), bank[0][:, 0:CHUNKS * E].rearrange("p (t e) -> p t e", t=CHUNKS),
                                        ALU.mult, ALU.add))
            then(V.tensor_tensor(pick[:], pick[:], onehot[:], ALU.mult))
            then(V.tensor_reduce(slot[:], pick[:], AX_X, ALU.add))
            then(V.tensor_copy(slot_i[:], slot[:]))
            then(V.tensor_scalar(lo_i[:], slot_i[:], P - 1, None, ALU.bitwise_and))
            V.tensor_copy(lo[:], lo_i[:]).then_inc(lo_ready, 1)
            then(V.tensor_scalar(hi_i[:], slot_i[:], 7, None, ALU.logical_shift_right))
            then(V.tensor_copy(hi[:], hi_i[:]))
            dve.wait_ge(lo_ready, 1)
            then(V.tensor_tensor(hi_hot[:],
                                 iota_p[:, 0:TILES].rearrange("p (a n) -> p a n", a=1).broadcast_to([P, CHUNKS, TILES]),
                                 hi[:].rearrange("p (t a) -> p t a", a=1).broadcast_to([P, CHUNKS, TILES]),
                                 ALU.is_equal))
            V.tensor_scalar(mov[:, :, 0], hi_hot[:], part1[:], None, ALU.mult).then_inc(mov_done, 1)
            V.tensor_tensor(mov[:, :, 1], hi_hot[:],
                            tval[:].rearrange("p (t a) -> p t a", a=1).broadcast_to([P, CHUNKS, TILES]),
                            ALU.mult).then_inc(mov_done, 1)
            def tile_expert(n):
                if n == 0:
                    V.tensor_tensor(ended[:], iota_p[:, 0:TILES].rearrange("p (n a) -> p n a", a=1).broadcast_to([P, TILES, E]),
                                    tend[:].rearrange("p (a e) -> p a e", a=1).broadcast_to([P, TILES, E]),
                                    ALU.is_ge).then_inc(route, 1)
                else:
                    dve.wait_ge(route, step_no[0])
                if n == 1:
                    V.tensor_reduce(expert_f[:], ended[:], AX_X, ALU.add).then_inc(route, 1)
                elif n == 2:
                    V.tensor_scalar(expert_f[:], expert_f[:], float(E - 1), None, ALU.min).then_inc(route, 1)
                elif n == 3:
                    V.tensor_copy(expert_i[:], expert_f[:]).then_inc(experts_ready, 1)
                step_no[0] += 1

            for t in range(LO_HOT_POOL):
                V.tensor_scalar(lo_hot[:, t], iota_b[:], lo[:, t:t + 1], None, ALU.is_equal
                                ).then_inc(lo_hot_done, 1)
                if 2 <= t < 6:
                    tile_expert(t - 2)
            step_no[0] -= 1
            dve.wait_ge(slots_done, 1)
            then(V.tensor_copy(slot_sb[:].rearrange("p a n -> p (a n)"), bank[2][:, 0:2 * TILES]))
            then(V.scalar_tensor_tensor(tok1[:], slot_sb[:, 1], float(P), slot_sb[:, 0], ALU.mult, ALU.add))
            then(V.tensor_scalar(gather_f[:], tok1[:], -1.0, 0.0, ALU.add, ALU.max))
            then(V.tensor_copy(gather_i[:], gather_f[:]))
            for j in range(4):
                V.tensor_copy(gidx[:, j:j + 1], gather_i[:, j:j + 1]).then_inc(first_gidx, 1)
            then(V.tensor_scalar(scatter_f[:], tok1[:], 0.0, float(2 * TOKENS), ALU.is_equal, ALU.mult))
            then(V.scalar_tensor_tensor(scatter_f[:], tok1[:], -1.0, scatter_f[:], ALU.add, ALU.add))
            then(V.tensor_copy(scatter_i[:], scatter_f[:]))

            def next_index(j, u):
                dve.wait_ge(xg_in[u % 4], 16 * (j // 4) if isinstance(j, int) else 4 * (j - u % 4))
                V.tensor_copy(gidx[:, u % 4:u % 4 + 1], gather_i[:, bass.ds(j, 1)]).then_inc(gidx_done, 1)

            def relu_h(j, u):
                dve.wait_ge(h_done, 2 * j + 2)
                dve.wait_ge(w1_in[u % 2], 16 * (j // 2 + 1) if isinstance(j, int) else 8 * (j - u % 2 + 2))
                if not (isinstance(j, int) and j < 1):
                    dve.wait_ge(h_low_pool, j)
                for f in range(4, FC):
                    V.tensor_scalar(hT[:, f], [bank[1], bank[3]][u % 2][:, (f - 4) * P:(f - 3) * P],
                                    w1s[:, u % 2, KC * F + f:KC * F + f + 1], 0.0, ALU.add, ALU.max
                                    ).then_inc(h_vec, 1)

            def finish(j, u):
                dve.wait_ge(y_done, j + 1)
                dve.wait_ge(b2_in[u % 4], 16 * (j // 4 + 1) if isinstance(j, int) else 4 * (j - u % 4 + 4))
                V.tensor_tensor(z2[:, u % 2], [bank[4], bank[5]][u % 2][:, 0:D], b2s[:, u % 4], ALU.add
                                ).then_inc(yb_done, 1)
                dve.wait_ge(yb_done, j + 1)
                dve.wait_ge(xg_in[u % 4], 16 * (j // 4 + 1) if isinstance(j, int) else 4 * (j - u % 4 + 4))
                V.scalar_tensor_tensor(z2[:, u % 2], z2[:, u % 2], xg[:, u % 4, D:D + 1], xg[:, u % 4, 0:D],
                                       ALU.mult, ALU.add).then_inc(z2_done, 1)
                dve.wait_ge(z2_done, j + 1)
                V.bn_stats(stats2[:], z2[:, u % 2]).then_inc(stats2_done, 1)
                dve.wait_ge(consts, 12)
                dve.wait_ge(stats2_done, j + 1)
                V.bn_aggr(mv2[:, u % 2], stats2[:]).then_inc(mv2_done, 1)

            def normalise2(j, u):
                dve.wait_ge(rstd2_done, j + 1)
                dve.wait_ge(mv2_done, j + 1)
                if not (isinstance(j, int) and j < 2):
                    dve.wait_ge(y_out[u % 2], 16 * (j // 2) if isinstance(j, int) else 8 * (j - u % 2))
                V.tensor_copy(sidx[:, u % 2:u % 2 + 1], scatter_i[:, bass.ds(j, 1)]).then_inc(sidx_done, 1)
                V.tensor_scalar(yo[:, u % 2], z2[:, u % 2], mv2[:, u % 2, 0:1], rstd2[:, u % 2:u % 2 + 1],
                                ALU.subtract, ALU.mult).then_inc(yo_done, 1)

            def split_h(j, u):
                dve.wait_ge(h_high_done, 2 * j + 1)
                V.tensor_tensor(hT_low[:, u % 2, 0:4].rearrange("p f n -> p (f n)"),
                                hT[:, 0:4].rearrange("p f n -> p (f n)"),
                                hT_high[:, u % 2, 0:4].rearrange("p f n -> p (f n)").bitcast(F32),
                                ALU.subtract).then_inc(h_low_vec, 1)

            relu_h(0, 0)
            split_h(0, 0)

            def step(j, u):
                if not (isinstance(j, int) and j + 1 >= TILES):
                    relu_h(j + 1, u + 1)
                if not (isinstance(j, int) and j + 4 >= TILES):
                    next_index(j + 4, u)
                if not (isinstance(j, int) and j + 1 >= TILES):
                    split_h(j + 1, u + 1)
                finish(j, u)
                normalise2(j, u)

            tiles(dve, step)


R_CONSTS = 8
C_STEPS = 13
C_COUNTED = 11
C_SHIFTED = 3
WARM = [3, 9, 7, 18]
LO_HOT_POOL = 20


def kernel(**inputs):
    import numpy as np
    import concourse.bacc as bacc
    from concourse.bass_utils import run_bass_kernel_spmd as run

    x = np.ascontiguousarray(inputs["L0_attn_x"])
    w1 = np.asarray(inputs["L0_ffn_W1"])
    b1 = np.asarray(inputs["L0_ffn_b1"])
    arrays = {
        "x": x,
        "xT": np.ascontiguousarray(x.reshape(BATCH, BLOCKS, P, KC, P).transpose(1, 0, 4, 3, 2)),
        "w_qkv": np.ascontiguousarray(inputs["L0_attn_W_qkv"]),
        "w_out": np.ascontiguousarray(inputs["L0_attn_W_out"]),
        "w_gate": np.ascontiguousarray(inputs["L0_ffn_w_gate"]),
        "b_gate": np.ascontiguousarray(inputs["L0_ffn_b_gate"]),
        "w1b": np.ascontiguousarray(np.concatenate([
            w1.reshape(E, KC, P, F).transpose(0, 2, 1, 3).reshape(E, P, KC * F),
            b1.reshape(E, FC, P).transpose(0, 2, 1)], axis=2)),
        "w2": np.ascontiguousarray(inputs["L0_ffn_W2"]),
        "b2": np.ascontiguousarray(inputs["L0_ffn_b2"]),
    }
    nc = bacc.Bacc("TRN2", target_bir_lowering=False, num_devices=1)
    args = [nc.dram_tensor(n, a.shape, mybir.dt.from_np(a.dtype), kind="ExternalInput").ap()
            for n, a in arrays.items()]
    out = nc.dram_tensor("out", (BATCH, SEQ, D), F32, kind="ExternalOutput").ap()
    attention_moe(nc, *args, out)
    r = run(nc, [arrays], core_ids=[0])
    return r.results[0]["out"]
```

```python
from contextlib import ExitStack

import concourse.bass as bass
from concourse import mybir

ALU = mybir.AluOpType
ACT = mybir.ActivationFunctionType
F32 = mybir.dt.float32
F32R = mybir.dt.float32r
BF16 = mybir.dt.bfloat16
I32 = mybir.dt.int32
U32 = mybir.dt.uint32
AX_X = mybir.AxisListType.X

P = 128
BATCH, SEQ, D = 4, 1024, 256
HEADS, HD = 16, 16
HV = HD + 1
E, F = 8, 1024
TOKENS = BATCH * SEQ
CHUNKS = TOKENS // P
BLOCKS = SEQ // P
KC = D // P
FC = F // P
TILES = CHUNKS + E - 1
HALF = HEADS // KC
PRODUCTS = [(0, 0), (0, 1), (1, 0)]
ROW_TILES = [(0, 2), (1, 3)]
EARLY_GROUPS = 5
EARLY = 4 * EARLY_GROUPS
EARLY_TILES = EARLY - (E - 1)
LATE_TILES = TILES - EARLY_TILES
STRAIGHT = 12
C_STEPS = 13
CHOICE_AT = [[[1], [2], [3], [4], [5]], [[6], [7], [8, 9], [10, 11], [12, 13]]]
C_SHIFTED = 3
C_PROBABLE = 7
EARLY_STEPS = 24
EARLY_READ = 6
R_CONSTS = 10
R_COUNTS = R_CONSTS + 1
R_FOUND = R_COUNTS + 20
LATE_STEPS = 23 + CHUNKS
TABLE_STEP = 8
KEEP_CLOCK = [3, 9, 7, 18]
W2_PIECE = FC * D // BATCH
assert E == BLOCKS
LN_EPS = 1e-5
DEN_EPS = 1e-6
W1_ROW = KC * F + FC


def attention_moe(nc, x, xT, w_qkv, w_out, w_gate, b_gate, w1b, w2, b2, out):
    with ExitStack() as ctx:
        def sb(name, shape, dt=F32):
            return ctx.enter_context(nc.sbuf_tensor(name, shape, dt))

        attention = ExitStack()

        def sa(name, shape, dt=F32):
            return attention.enter_context(nc.sbuf_tensor(name, shape, dt))

        def sem(name):
            return ctx.enter_context(nc.semaphore(name))

        x1_rows = nc.dram_tensor("x1_rows", (TOKENS, D + 1), F32, kind="Internal").ap()

        bg = sb("bg", [P, E])
        w2_high = sb("w2_high", [P, E * FC * D], F32R)
        w2_low = sb("w2_low", [P, E * FC * D], F32R)
        ident = sb("ident", [P, P])
        iota_i = sb("iota_i", [P, P], I32)
        ln_power = sb("ln_power", [P, 1])
        ln_eps = sb("ln_eps", [P, 1])
        lg = sb("lg", [P, 4, E])
        rank8 = sb("rank8", [P, E])
        before_b = sb("before_b", [P, P], BF16)
        ones_b = sb("ones_b", [P, P], BF16)
        hi_i = sb("hi_i", [P, CHUNKS], I32)
        lo_i = sb("lo_i", [P, CHUNKS], I32)
        iota_p = sb("iota_p", [P, P])
        iota_b = sb("iota_b", [P, P], BF16)
        part1_i = sb("part1_i", [P, 1], I32)
        part1 = sb("part1", [P, 1])
        tval_i = sb("tval_i", [P, CHUNKS], I32)
        tval = sb("tval", [P, CHUNKS])
        lmax = sb("lmax", [P, 4])
        ex = sb("ex", [P, 4, E])
        esum = sb("esum", [P, 4])
        top_p = sb("top_p", [P, CHUNKS])
        hit = sb("hit", [P, 4, E])
        first_hit = sb("first_hit", [P, 4])
        onehot = sb("onehot", [P, 4, E])
        onehot_b = sb("onehot_b", [P, CHUNKS * E], BF16)
        prefix_b = sb("prefix_b", [P, (CHUNKS + 1) * E], BF16)
        ones_e = sb("ones_e", [P, E])
        tile_end = sb("tile_end", [P, 1 + E])
        early_n = sb("early_n", [P, E])
        taken = sb("taken", [P, CHUNKS])
        gather_f = sb("gather_f", [P, TILES])
        gather_i = sb("gather_i", [P, TILES], U32)
        scatter_i = sb("scatter_i", [P, TILES], U32)
        expert_f = sb("expert_f", [P, TILES])
        expert_i = sb("expert_i", [P, TILES], I32)
        tok1 = sb("tok1", [P, TILES])
        slot = sb("slot", [P, CHUNKS])
        slot_i = sb("slot_i", [P, CHUNKS], I32)
        hi = sb("hi", [P, CHUNKS])
        lo = sb("lo", [P, CHUNKS])
        count_i = sb("count_i", [P, E], I32)
        tiles_i = sb("tiles_i", [P, E], I32)
        ntile = sb("ntile", [P, E])
        gidx = sb("gidx", [P, 4], U32)
        xt = sa("xt", [P, BATCH, KC, P])
        wqk = sa("wqk", [P, KC, 2 * D])
        wv_part = sa("wv_part", [P, 2, KC, D], F32R)
        x_part = sa("x_part", [P, 2, KC, P], F32R)
        expo = sa("expo", [P, 4 * P])
        relu = sa("relu", [P, 4 * P])
        xn = sa("xn", [P, BATCH, D])
        phi = sa("phi", [P, 2, 4, P])
        q_part = sa("q_part", [P, 2, KC, 2, P], F32R)
        k_part = sa("k_part", [P, 2, KC, P], F32R)
        vext = sa("vext", [P, 2, HEADS * HV + 16])
        kn = sa("kn", [P, D])
        probs = sa("probs", [P, 4, 4, P])
        avt = sa("avt", [P, 4, P])
        state = sa("state", [P, BATCH, KC, HALF * HV])
        state_add = sa("state_add", [P, KC, HALF * HV])
        den = sa("den", [P, HEADS])
        rden = sa("rden", [P, HEADS])
        att = sa("att", [P, D])
        attT = sa("attT", [P, 2, KC, P], F32R)
        z = sa("z", [P, 2, D])
        stats = sa("stats", [P, 6])
        mv = sa("mv", [P, 2, 2])
        veps = sa("veps", [P, 2])
        rstd = sa("rstd", [P, 2])
        x1 = sa("x1", [P, BATCH, D])
        x1T = sa("x1T", [P, KC, P])
        wo_part = sa("wo_part", [P, 2, KC, D], F32R)
        wg = sa("wg", [P, KC, E])
        causal = sa("causal", [P, P])
        select = sa("select", [P, 4 * HV])
        diag = sa("diag", [P, HALF, HV])
        parity = sa("parity", [P, 2])
        w2_raw = sa("w2_raw", [P, W2_PIECE])
        early_lo_hot = sa("early_lo_hot", [P, EARLY // 2, P], BF16)
        early_hi_hot = sa("early_hi_hot", [P, EARLY, EARLY_TILES], BF16)
        early_mov = sa("early_mov", [P, EARLY, 2, EARLY_TILES], BF16)
        early_pick = sa("early_pick", [P, EARLY, E])
        early_limit = sa("early_limit", [P, EARLY])
        early_slots = sa("early_slots", [P, 2, EARLY_TILES])
        early_ended = (early_pick[:].rearrange("p t e -> p (t e)")[:, 0:EARLY_TILES * E]
                       .rearrange("p (t e) -> p t e", e=E))
        attention.close()
        w1s = sb("w1s", [P, 2, W1_ROW])
        pick = sb("pick", [P, CHUNKS, E])
        tstart = sb("tstart", [P, E])
        shift = sb("shift", [P, E])
        offset = sb("offset", [P, CHUNKS])
        tend = sb("tend", [P, E])
        lo_hot = sb("lo_hot", [P, CHUNKS, P], BF16)
        hi_hot = sb("hi_hot", [P, CHUNKS, LATE_TILES], BF16)
        mov = sb("mov", [P, CHUNKS, 2, LATE_TILES], BF16)
        slot_sb = sb("slot_sb", [P, 2, LATE_TILES])
        scatter_f = sb("scatter_f", [P, LATE_TILES])
        ended = sb("ended", [P, LATE_TILES, E])
        b2s = sb("b2s", [P, 4, D])
        sidx = sb("sidx", [P, 2], U32)
        xg = sb("xg", [P, 4, D + 1])
        xgT = sb("xgT", [P, 2, KC, P])
        hT_high = sb("hT_high", [P, 2, FC, P], F32R)
        hT_low = sb("hT_low", [P, 2, FC, P], F32R)
        hT = sb("hT", [P, FC, P])
        z2 = sb("z2", [P, 2, D])
        stats2 = sb("stats2", [P, 6])
        mv2 = sb("mv2", [P, 2, 2])
        veps2 = sb("veps2", [P, 2])
        rstd2 = sb("rstd2", [P, 2])
        yo = sb("yo", [P, 2, D])

        bank = [ctx.enter_context(nc.psum_tensor(f"bank{i}", [P, 512], F32)) for i in range(8)]
        b_av, b_nat, b_kv, b_op = bank[0], bank[1], bank[2], bank[3]
        b_qk, b_vk, b_tr, b_lg = bank[4], bank[5], bank[6], bank[7]

        raw = probs[:].rearrange("p r j n -> p (r j n)").rearrange("p (w c n) -> p w c n", w=4, c=KC)

        early_sums = [b_lg[:, 432 + 2 * EARLY_TILES * h:432 + 2 * EARLY_TILES * (h + 1)] for h in range(2)]

        w_in = sem("w_in")
        w2_in = sem("w2_in")
        wvo_in = sem("wvo_in")
        xt_in = [sem(f"xt_in{b}") for b in range(BATCH)]
        xn_in = [sem(f"xn_in{b}") for b in range(BATCH)]
        x1_out = [sem(f"x1_out{b}") for b in range(BATCH)]
        zeroed = sem("zeroed")
        consts = sem("consts")
        iotas = sem("iotas")
        vec_consts = sem("vec_consts")
        qk_done = sem("qk_done")
        v_done = sem("v_done")
        er_done = sem("er_done")
        v_evac = sem("v_evac")
        phi_done = sem("phi_done")
        high_done = sem("high_done")
        q_low_done = sem("q_low_done")
        k_low_done = sem("k_low_done")
        kn_done = sem("kn_done")
        kn_evac = sem("kn_evac")
        sc_done = sem("sc_done")
        probs_done = sem("probs_done")
        av_done = sem("av_done")
        av_evac = sem("av_evac")
        nat_done = sem("nat_done")
        den_done = sem("den_done")
        rden_done = sem("rden_done")
        att_done = sem("att_done")
        kv_done = sem("kv_done")
        kv_masked = sem("kv_masked")
        state_done = sem("state_done")
        attT_done = sem("attT_done")
        attT_evac = sem("attT_evac")
        attT_low = sem("attT_low")
        w_high = sem("w_high")
        w_low = sem("w_low")
        x_high = sem("x_high")
        x_low = sem("x_low")
        op_done = sem("op_done")
        z_done = sem("z_done")
        stats_done = sem("stats_done")
        mv_done = sem("mv_done")
        veps_done = sem("veps_done")
        rstd_done = sem("rstd_done")
        x1_done = sem("x1_done")
        x1T_done = sem("x1T_done")
        x1T_evac = sem("x1T_evac")
        lg_done = sem("lg_done")
        route = sem("route")
        choice = sem("choice")
        exp_done = sem("exp_done")
        p_out = sem("p_out")
        early = sem("early")
        early_counted = sem("early_counted")
        early_lo = sem("early_lo")
        early_half = sem("early_half")
        early_done = sem("early_done")
        rank_read = sem("rank_read")
        slots_read = sem("slots_read")
        count_done = sem("count_done")
        lo_hot_done = sem("lo_hot_done")
        mov_done = sem("mov_done")
        slots_done = sem("slots_done")
        experts_ready = sem("experts_ready")
        idx_ready = sem("idx_ready")
        w1_in = [sem(f"w1_in{b}") for b in range(2)]
        b2_in = [sem(f"b2_in{b}") for b in range(4)]
        xg_in = [sem(f"xg_in{b}") for b in range(4)]
        y_out = [sem(f"y_out{b}") for b in range(2)]
        first_gidx = sem("first_gidx")
        gidx_done = sem("gidx_done")
        sidx_done = sem("sidx_done")
        xgT_done = sem("xgT_done")
        xgT_evac = sem("xgT_evac")
        h_done = sem("h_done")
        w2_high_done = sem("w2_high_done")
        w2_low_done = sem("w2_low_done")
        h_high_done = sem("h_high_done")
        h_low_vec = sem("h_low_vec")
        h_low_pool = sem("h_low_pool")
        h_act = sem("h_act")
        h_vec = sem("h_vec")
        y_done = sem("y_done")
        yb_done = sem("yb_done")
        z2_done = sem("z2_done")
        stats2_done = sem("stats2_done")
        mv2_done = sem("mv2_done")
        veps2_done = sem("veps2_done")
        rstd2_done = sem("rstd2_done")
        yo_done = sem("yo_done")

        block = ctx.enter_context(nc.Block())

        def groups(eng, body):
            body(0, True, False)
            with eng.Fori(1, BLOCKS - 1) as i:
                body(i, False, False)
            body(BLOCKS - 1, False, True)

        def tiles(eng, body, straight=4, before_late=None):
            for j in range(straight):
                body(j, j % 4)
            if straight < STRAIGHT:
                with eng.Fori(straight // 4, STRAIGHT // 4) as k:
                    for u in range(4):
                        body(4 * k + u, u)
            if before_late is not None:
                before_late()
            with eng.Fori(STRAIGHT // 4, TILES // 4 - 1) as k:
                for u in range(4):
                    body(4 * k + u, u)
            for j in range((TILES // 4 - 1) * 4, TILES):
                body(j, j % 4)

        @block.sync
        def _(sp):
            w_rows = w_qkv.rearrange("(c p) n -> p c n", p=P)
            sp.dma_start(wqk[:], w_rows[:, :, 0:2 * D]).then_inc(w_in, 16)

            def load(t, i, b):
                sp.dma_start(xt[:, b], xT[bass.ds(i, 1), b].rearrange("a p c n -> (a p) c n")
                             ).then_inc(xt_in[b], 16)
                sp.dma_start(xn[:, b], x[b, bass.ds(i * P, P), :]).then_inc(xn_in[b], 16)

            for b in range(BATCH):
                load(b, 0, b)
                if b == 0:
                    sp.dma_start(raw[:, 0], w_rows[:, :, 2 * D:3 * D]).then_inc(wvo_in, 16)
                    sp.dma_start(raw[:, 1], w_out.rearrange("(c p) n -> p c n", p=P)).then_inc(wvo_in, 16)
                    sp.dma_start(wg[:], w_gate.rearrange("(c p) n -> p c n", p=P)).then_inc(w_in, 16)
                    sp.dma_start(bg[:], b_gate.rearrange("(a e) -> a e", a=1).broadcast_to([P, E])
                                 ).then_inc(w_in, 16)

            def store_x1(t, i, b):
                sp.wait_ge(x1_done, t + 1)
                sp.dma_start(x1_rows[bass.ds(b * SEQ + i * P, P), 0:D], x1[:, b]
                             ).then_inc(x1_out[b], 16)

            with sp.Fori(1, BLOCKS) as i:
                for b in range(BATCH):
                    t = 4 * i + b
                    sp.wait_ge(qk_done, t - 3)
                    sp.wait_ge(x_low, t - 3)
                    sp.wait_ge(z_done, t - 3)
                    load(t, i, b)
                    store_x1(t - 4, i - 1, b)
            def load_w1(j, u):
                if not (isinstance(j, int) and j < 2):
                    sp.wait_ge(h_act, 4 * (j - 1))
                    sp.wait_ge(h_vec, 4 * (j - 1))
                e = sp.value_load(expert_i[0:1, bass.ds(j, 1)], min_val=0, max_val=E - 1)
                sp.dma_start(w1s[:, u % 2], w1b[bass.ds(e, 1)].rearrange("a p n -> (a p) n")
                             ).then_inc(w1_in[u % 2], 16)

            def load_b2(j, u):
                e = sp.value_load(expert_i[0:1, bass.ds(j, 1)], min_val=0, max_val=E - 1)
                if not (isinstance(j, int) and j < 4):
                    sp.wait_ge(yb_done, j - 3)
                sp.dma_start(b2s[:, u % 4], b2[bass.ds(e, 1), :].broadcast_to([P, D])
                             ).then_inc(b2_in[u % 4], 16)

            store_x1(CHUNKS - 4, BLOCKS - 1, 0)
            store_x1(CHUNKS - 3, BLOCKS - 1, 1)
            sp.wait_ge(experts_ready, 1)
            sp.wait_ge(v_done, CHUNKS)
            sp.wait_ge(phi_done, CHUNKS)
            load_w1(0, 0)
            load_w1(1, 1)
            store_x1(CHUNKS - 2, BLOCKS - 1, 2)
            store_x1(CHUNKS - 1, BLOCKS - 1, 3)
            sp.wait_ge(lg_done, CHUNKS)
            load_b2(0, 0)
            load_b2(1, 1)

            def load(j, u):
                if not (isinstance(j, int) and j < 2):
                    load_w1(j, u)
                    load_b2(j, u)

            tiles(sp, load, before_late=lambda: sp.wait_ge(experts_ready, 2))

        @block.gpsimd
        def _(pool):
            nc.gpsimd.memset(causal[:], 1.0).then_inc(zeroed, 1)
            nc.gpsimd.memset(ident[:], 0.0).then_inc(zeroed, 1)
            nc.gpsimd.memset(select[:], 0.0).then_inc(zeroed, 1)
            nc.gpsimd.memset(diag[:], 1.0).then_inc(zeroed, 1)
            nc.gpsimd.memset(before_b[:], 1.0).then_inc(zeroed, 1)
            nc.gpsimd.memset(ln_power[:], -0.5).then_inc(consts, 1)
            nc.gpsimd.memset(ln_eps[:], LN_EPS).then_inc(consts, 1)
            nc.gpsimd.memset(ones_b[:], 1.0).then_inc(consts, 1)
            nc.gpsimd.memset(ones_e[:], 1.0).then_inc(consts, 1)
            pool.wait_ge(zeroed, 5)
            sel = nc.gpsimd.affine_select
            sel(out=causal[:], in_=causal[:], compare_op=ALU.is_ge, fill=0.0, base=0,
                pattern=[[1, P]], channel_multiplier=-1).then_inc(consts, 1)
            sel(out=before_b[:], in_=before_b[:], compare_op=ALU.is_gt, fill=0.0, base=0,
                pattern=[[1, P]], channel_multiplier=-1).then_inc(consts, 1)
            sel(out=ident[:], in_=ident[:], compare_op=ALU.not_equal, fill=1.0, base=0,
                pattern=[[-1, P]], channel_multiplier=1).then_inc(consts, 1)
            for j in range(4):
                v = select[:, HV * j:HV * (j + 1)]
                sel(out=v, in_=v, compare_op=ALU.not_equal, fill=1.0, base=-32 * j,
                    pattern=[[-1, HV]], channel_multiplier=1).then_inc(consts, 1)
            sel(out=diag[:], in_=diag[:], compare_op=ALU.is_ge, fill=0.0, base=0,
                pattern=[[-HD, HALF], [0, HV]], channel_multiplier=1).then_inc(zeroed, 1)
            pool.wait_ge(zeroed, 6)
            sel(out=diag[:], in_=diag[:], compare_op=ALU.is_ge, fill=0.0, base=HD - 1,
                pattern=[[HD, HALF], [0, HV]], channel_multiplier=-1).then_inc(consts, 1)
            nc.gpsimd.iota(part1_i[:], pattern=[[0, 1]], base=1, channel_multiplier=1).then_inc(iotas, 1)
            nc.gpsimd.iota(tval_i[:], pattern=[[1, BLOCKS], [BLOCKS, BATCH]], base=0,
                           channel_multiplier=0).then_inc(iotas, 1)
            nc.gpsimd.iota(iota_i[:], pattern=[[1, P]], base=0, channel_multiplier=0).then_inc(iotas, 1)

            def split_x(t, b):
                pool.wait_ge(x_high, t + 1)
                nc.gpsimd.tensor_tensor(x_part[:, 1].rearrange("p c n -> p (c n)"),
                                        xt[:, b].rearrange("p c n -> p (c n)"),
                                        x_part[:, 0].rearrange("p c n -> p (c n)").bitcast(F32),
                                        ALU.subtract).then_inc(x_low, 1)

            def k_low(t, par):
                pool.wait_ge(high_done, 3 * t + 1)
                nc.gpsimd.tensor_tensor(k_part[:, 1].rearrange("p c n -> p (c n)"),
                                        phi[:, par, 2:4].rearrange("p c n -> p (c n)"),
                                        k_part[:, 0].rearrange("p c n -> p (c n)").bitcast(F32),
                                        ALU.subtract).then_inc(k_low_done, 1)

            def add_state(t, b):
                pool.wait_ge(kv_masked, t + 1)
                pool.wait_ge(nat_done, t + 1)
                nc.gpsimd.tensor_tensor(state[:, b], state[:, b], state_add[:], ALU.add
                                        ).then_inc(state_done, 1)

            def power(t, par):
                pool.wait_ge(mv_done, t + 1)
                nc.gpsimd.tensor_tensor(veps[:, par:par + 1], mv[:, par, 1:2], ln_eps[:], ALU.add
                                        ).then_inc(veps_done, 1)
                pool.wait_ge(veps_done, t + 1)
                nc.gpsimd.tensor_tensor(rstd[:, par:par + 1], veps[:, par:par + 1], ln_power[:], ALU.pow
                                        ).then_inc(rstd_done, 1)

            def split_w2(e, u):
                pool.wait_ge(w2_high_done, 4 * e + u + 1)
                piece = bass.ds((4 * e + u) * W2_PIECE, W2_PIECE)
                nc.gpsimd.tensor_tensor(w2_low[:, piece], w2_raw[:],
                                        w2_high[:, piece].bitcast(F32), ALU.subtract).then_inc(w2_low_done, 1)

            split_x(0, 0)
            k_low(0, 0)
            split_x(1, 1)

            def group(i, first, last):
                for u in range(4):
                    t = 4 * i + u
                    if not (first and u == 0):
                        split_w2(i - 1 if u == 0 else i, (u + 3) % 4)
                    if not (last and u == 3):
                        k_low(t + 1, (u + 1) % 2)
                    add_state(t, u)
                    if not (first and u == 0):
                        power(t - 1, (u + 1) % 2)
                    if not (last and u >= 2):
                        split_x(t + 2, (u + 2) % 4)

            groups(pool, group)
            power(CHUNKS - 1, (CHUNKS - 1) % 2)
            split_w2(E - 1, 3)

            for b in range(BATCH):
                pool.wait_ge(x1_out[b], 16 * BLOCKS)
            pool.wait_ge(p_out, 16 * BLOCKS)

            def gather(j, u, met):
                pool.wait_ge(consts, 12)
                if isinstance(j, int) and j < 4:
                    pool.wait_ge(first_gidx, j + 1)
                else:
                    pool.wait_ge(gidx_done, met)
                    pool.wait_ge(z2_done, met)
                nc.gpsimd.indirect_dma_start(
                    out=xg[:, u % 4], out_offset=None, in_=x1_rows,
                    in_offset=bass.IndirectOffsetOnAxis(ap=gidx[:, u % 4:u % 4 + 1], axis=0),
                    bounds_check=TOKENS - 1, oob_is_err=False).then_inc(xg_in[u % 4], 16)

            for j in range(4):
                gather(j, j, 0)

            def split_h(j, u):
                pool.wait_ge(h_high_done, 2 * j + 2)
                nc.gpsimd.tensor_tensor(hT_low[:, u % 2, 4:FC].rearrange("p f n -> p (f n)"),
                                        hT[:, 4:FC].rearrange("p f n -> p (f n)"),
                                        hT_high[:, u % 2, 4:FC].rearrange("p f n -> p (f n)").bitcast(F32),
                                        ALU.subtract).then_inc(h_low_pool, 1)

            split_h(0, 0)

            def tile_j(j, u):
                if not (isinstance(j, int) and j + 1 >= TILES):
                    split_h(j + 1, u + 1)
                pool.wait_ge(mv2_done, j + 1)
                nc.gpsimd.tensor_tensor(veps2[:, u % 2:u % 2 + 1], mv2[:, u % 2, 1:2], ln_eps[:],
                                        ALU.add).then_inc(veps2_done, 1)
                pool.wait_ge(veps2_done, j + 1)
                nc.gpsimd.tensor_tensor(rstd2[:, u % 2:u % 2 + 1], veps2[:, u % 2:u % 2 + 1],
                                        ln_power[:], ALU.pow).then_inc(rstd2_done, 1)
                if not (isinstance(j, int) and j + 4 >= TILES):
                    gather(j + 4, u, j + 1)
                pool.wait_ge(consts, 12)
                pool.wait_ge(yo_done, j + 1)
                pool.wait_ge(sidx_done, j + 1)
                nc.gpsimd.indirect_dma_start(
                    out=out.rearrange("b s d -> (b s) d"),
                    out_offset=bass.IndirectOffsetOnAxis(ap=sidx[:, u % 2:u % 2 + 1], axis=0),
                    in_=yo[:, u % 2], in_offset=None,
                    bounds_check=TOKENS - 1, oob_is_err=False).then_inc(y_out[u % 2], 16)

            tiles(pool, tile_j)
            pool.wait_ge(y_out[0], 16 * ((TILES + 1) // 2))
            pool.wait_ge(y_out[1], 16 * (TILES // 2))

        @block.tensor
        def _(pe):
            mm = nc.tensor.matmul

            def scores_and_qk(t, par, more, b, i):
                pe.wait_ge(q_low_done, 2 * (t + 1))
                pe.wait_ge(k_low_done, t + 1)
                for n, pair in enumerate(ROW_TILES):
                    if not (isinstance(t, int) and t == 0):
                        pe.wait_ge([av_evac, att_done][n], t)
                        if n == 0:
                            pe.wait_ge(kv_masked, t)
                    if n == 1 and not (isinstance(t, int) and t < 2):
                        pe.wait_ge(z_done, t - 1)
                    for c in range(KC):
                        for kp, qp in PRODUCTS:
                            for r in pair:
                                rows = slice(32 * r, 32 * r + 32)
                                m = mm(bank[r][:, 2 * c * P:2 * (c + 1) * P], k_part[rows, kp, c, :],
                                       q_part[rows, qp, c].rearrange("p e n -> p (e n)"),
                                       start=(kp + qp == 0), stop=(kp == 1))
                    m.then_inc(sc_done, 1)
                    if more:
                        project_qk(t + 1, b, i, [n])
                if more:
                    project_qk(t + 1, b, i, [2, 3])

            def project_qk(t, b, i, slices):
                if slices[0] == 0:
                    pe.wait_ge(xt_in[b], 16 * (i + 1))
                    if not (isinstance(t, int) and t == 0):
                        pe.wait_ge(er_done, 2 * t)
                for s in slices:
                    for c in range(KC):
                        m = mm(b_qk[:, s * P:(s + 1) * P], wqk[:, c, s * P:(s + 1) * P], xt[:, b, c],
                               start=(c == 0), stop=(c == KC - 1))
                if slices[-1] == 3:
                    m.then_inc(qk_done, 1)

            def project_v(t, b):
                if not (isinstance(t, int) and t == 0):
                    pe.wait_ge(kn_evac, t)
                pe.wait_ge(x_low, t + 1)
                for c in range(KC):
                    for xp, wp in PRODUCTS:
                        m = mm(b_vk[:, 0:D], x_part[:, xp, c], wv_part[:, wp, c],
                               start=(c == 0 and xp + wp == 0), stop=(c == KC - 1 and xp == 1))
                m.then_inc(v_done, 1)

            def k_rows(t, par):
                pe.wait_ge(phi_done, t + 1)
                pe.wait_ge(v_evac, t + 1)
                for c in range(KC):
                    m = nc.tensor.transpose(b_vk[:, c * P:(c + 1) * P], phi[:, par, 2 + c], ident[:])
                m.then_inc(kn_done, 1)

            def own_values(t, par):
                for n, r in enumerate(ROW_TILES[0] + ROW_TILES[1]):
                    pe.wait_ge(probs_done, 4 * t + n + 1)
                    if n == 0:
                        pe.wait_ge(v_evac, t + 1)
                    for j in range(4):
                        head = HALF * (j // 2) + 2 * r + j % 2
                        m = mm(b_av[32 * j:32 * j + 32, r * P:(r + 1) * P], vext[:, par, HV * head:HV * head + 32],
                               probs[:, r, j], start=True, stop=True)
                m.then_inc(av_done, 1)

            def chunk_state(t, par):
                pe.wait_ge(kn_evac, t + 1)
                for c in range(KC):
                    m = mm(b_kv[:, c * HALF * HV:(c + 1) * HALF * HV], kn[:, c * P:(c + 1) * P],
                           vext[:, par, HALF * c * HV:HALF * (c + 1) * HV], start=True, stop=True)
                m.then_inc(kv_done, 1)

            def numerators(t, b, par):
                if not (isinstance(t, int) and t < 4):
                    pe.wait_ge(state_done, t - 3)
                for c in range(KC):
                    mm(b_nat[:, c * HALF * HV:(c + 1) * HALF * HV], phi[:, par, c], state[:, b, c],
                       start=(c == 0), stop=False, skip_group_check=True)
                pe.wait_ge(av_evac, t + 1)
                nat = b_nat[:, 0:HEADS * HV].rearrange("p (c r n) -> p c r n", c=KC, r=4)
                for r in range(4):
                    m = mm(nat[:, :, r], avt[:, r], select[:].rearrange("p (c n) -> p c n", c=KC),
                           start=False, stop=(r == 3), skip_group_check=True)
                m.then_inc(nat_done, 1)

            def att_transpose(t):
                pe.wait_ge(att_done, t + 1)
                if not (isinstance(t, int) and t < 2):
                    pe.wait_ge(x1T_evac, t - 1)
                for c in range(KC):
                    m = nc.tensor.transpose(b_tr[:, c * P:(c + 1) * P], att[:, c * P:(c + 1) * P], ident[:])
                m.then_inc(attT_done, 1)

            def project_out(t):
                pe.wait_ge(attT_low, t + 1)
                if not (isinstance(t, int) and t == 0):
                    pe.wait_ge(z_done, t)
                for c in range(KC):
                    for ap, wp in PRODUCTS:
                        m = mm(b_op[:, 0:D], attT[:, ap, c], wo_part[:, wp, c],
                               start=(c == 0 and ap + wp == 0), stop=(c == KC - 1 and ap == 1))
                m.then_inc(op_done, 1)

            def x1_transpose(t, b):
                pe.wait_ge(x1_done, t + 1)
                if isinstance(t, int) and t == CHUNKS - 1:
                    pe.wait_ge(x1T_evac, t)
                else:
                    pe.wait_ge(attT_low, t + 2)
                for c in range(KC):
                    m = nc.tensor.transpose(b_tr[:, c * P:(c + 1) * P], x1[:, b, c * P:(c + 1) * P], ident[:])
                m.then_inc(x1T_done, 1)

            def early_counts():
                pe.wait_ge(choice, C_STEPS * EARLY_GROUPS)
                w = EARLY * E
                mm(b_lg[:, 256:256 + E], ones_b[:], prefix_b[:, w:w + E], start=True, stop=True)
                mm(b_lg[:, 264:264 + w], before_b[:], onehot_b[:, 0:w], start=True, stop=False)
                mm(b_lg[:, 264:264 + w], ones_b[:], prefix_b[:, 0:w], start=False, stop=True
                   ).then_inc(early_counted, 1)

            def early_table(half):
                for t in range(EARLY // 2 * half, EARLY // 2 * (half + 1)):
                    pe.wait_ge(early_lo, t + 1)
                    m = mm(early_sums[half], early_lo_hot[:, t % (EARLY // 2)],
                           early_mov[:, t].rearrange("p a n -> p (a n)"), start=(t % (EARLY // 2) == 0),
                           stop=((t + 1) % (EARLY // 2) == 0))
                m.then_inc(early_half, 1)

            def logits(t, read=None):
                pe.wait_ge(x1T_evac, t + 1)
                if read is not None:
                    pe.wait_ge(choice, C_STEPS * (read - 1) + 1)
                for c in range(KC):
                    m = mm(b_lg[:, bass.ds(t * E, E)], x1T[:, c], wg[:, c], start=(c == 0), stop=(c == KC - 1))
                m.then_inc(lg_done, 1)

            def keep_clock(n, into=b_lg):
                for _ in range(n):
                    mm(into[:, 256:384], ident[:], ident[:], start=True, stop=True)

            pe.wait_ge(consts, 12)
            keep_clock(KEEP_CLOCK[0])
            pe.wait_ge(w_in, 16)
            project_qk(0, 0, 0, range(4))
            keep_clock(KEEP_CLOCK[1])
            pe.wait_ge(w_low, 2)
            project_v(0, 0)
            k_rows(0, 0)
            keep_clock(KEEP_CLOCK[2])
            pe.wait_ge(w_in, 48)

            def group(i, first, last):
                for u in range(4):
                    t, par = 4 * i + u, u % 2
                    more = not (last and u == 3)
                    if last and u == 0:
                        pe.wait_ge(choice, C_STEPS * (BLOCKS - 2))
                        early_counts()
                    scores_and_qk(t, par, more, (u + 1) % 4, i + (u + 1) // 4)
                    if more:
                        project_v(t + 1, (u + 1) % 4)
                    if not (first and u < 1):
                        att_transpose(t - 1)
                    own_values(t, par)
                    chunk_state(t, par)
                    numerators(t, u, par)
                    if not (first and u < 2):
                        x1_transpose(t - 2, (u + 2) % 4)
                    if not (first and u < 1):
                        project_out(t - 1)
                    if more:
                        k_rows(t + 1, (u + 1) % 2)
                    if last and u == 0:
                        pe.wait_ge(early, EARLY_READ)
                    if last and u == 3:
                        pe.wait_ge(early, EARLY_STEPS + 1)
                    if not (first and u < 2):
                        logits(t - 2, None if first or u < 2 else i)
                    if last and u >= 2:
                        early_table(u - 2)

            groups(pe, group)
            att_transpose(CHUNKS - 1)
            project_out(CHUNKS - 1)
            x1_transpose(CHUNKS - 2, 2)
            pe.wait_ge(early_done, 1)
            logits(CHUNKS - 2)
            x1_transpose(CHUNKS - 1, 3)
            logits(CHUNKS - 1)
            keep_clock(KEEP_CLOCK[3], b_qk)

            def late_counts():
                pe.wait_ge(choice, C_STEPS * BLOCKS)
                mm(bank[5][:, 256:256 + E], ones_b[:], prefix_b[:, CHUNKS * E:], start=True, stop=True)
                mm(bank[5][:, 0:CHUNKS * E], before_b[:], onehot_b[:], start=True, stop=False)
                mm(bank[5][:, 0:CHUNKS * E], ones_b[:], prefix_b[:, 0:CHUNKS * E], start=False, stop=True
                   ).then_inc(count_done, 1)

            def late_table():
                pe.wait_ge(mov_done, 2)
                for t in range(CHUNKS):
                    pe.wait_ge(lo_hot_done, t + 1)
                    m = mm(bank[5][:, 0:2 * LATE_TILES], lo_hot[:, t], mov[:, t].rearrange("p a n -> p (a n)"),
                           start=(t == 0), stop=(t == CHUNKS - 1))
                m.then_inc(slots_done, 1)

            b_h = [[bank[0], bank[1]], [bank[2], bank[3]]]
            b_y = [bank[4], bank[5]]
            b_xt = [bank[6], bank[7]]

            def rows_transpose(j, u):
                pe.wait_ge(xg_in[u % 4], 16 * (j // 4 + 1) if isinstance(j, int) else 4 * (j - u % 4 + 4))
                if not (isinstance(j, int) and j < 2):
                    pe.wait_ge(xgT_evac, j - 1)
                for c in range(KC):
                    m = nc.tensor.transpose(b_xt[u % 2][:, c * P:(c + 1) * P],
                                            xg[:, u % 4, c * P:(c + 1) * P], ident[:])
                m.then_inc(xgT_done, 1)

            def hidden(j, u):
                pe.wait_ge(w1_in[u % 2], 16 * (j // 2 + 1) if isinstance(j, int) else 8 * (j - u % 2 + 2))
                pe.wait_ge(xgT_evac, j + 1)
                if not (isinstance(j, int) and j < 2):
                    pe.wait_ge(h_act, 4 * (j - 1))
                    pe.wait_ge(h_vec, 4 * (j - 1))
                for g in range(2):
                    for f in range(4):
                        for c in range(KC):
                            at = c * F + (4 * g + f) * P
                            m = mm(b_h[u % 2][g][:, f * P:(f + 1) * P], w1s[:, u % 2, at:at + P],
                                   xgT[:, u % 2, c], start=(c == 0), stop=(c == KC - 1))
                    m.then_inc(h_done, 1)

            def outputs(j, u):
                e = pe.value_load(expert_i[0:1, bass.ds(j, 1)], min_val=0, max_val=E - 1)
                if not (isinstance(j, int) and j < 2):
                    pe.wait_ge(yb_done, j - 1)
                for f in range(FC):
                    if f == 0:
                        pe.wait_ge(h_low_vec, j + 1)
                    if f == 4:
                        pe.wait_ge(h_low_pool, j + 1)
                    w = bass.ds(e * (FC * D) + f * D, D)
                    for hp, wp in PRODUCTS:
                        m = mm(b_y[u % 2][:, 0:D], [hT_high, hT_low][hp][:, u % 2, f], [w2_high, w2_low][wp][:, w],
                               start=(f == 0 and hp + wp == 0), stop=(f == FC - 1 and hp == 1))
                m.then_inc(y_done, 1)

            pe.wait_ge(w2_low_done, CHUNKS)
            pe.wait_ge(experts_ready, 1)
            rows_transpose(0, 0)
            rows_transpose(1, 1)
            hidden(0, 0)

            def step(j, u):
                if not (isinstance(j, int) and j + 1 >= TILES):
                    hidden(j + 1, u + 1)
                if not (isinstance(j, int) and j + 2 >= TILES):
                    rows_transpose(j + 2, u + 2)
                if isinstance(j, int) and j == 1:
                    pe.wait_ge(rank_read, 1)
                if isinstance(j, int) and j == TABLE_STEP + 1:
                    pe.wait_ge(slots_read, 1)
                outputs(j, u)
                if isinstance(j, int) and j == 0:
                    late_counts()
                if isinstance(j, int) and j == TABLE_STEP:
                    pe.wait_ge(yb_done, j)
                    late_table()

            tiles(pe, step, STRAIGHT, lambda: pe.wait_ge(experts_ready, 2))

        @block.scalar
        def _(act):
            def exp_relu(t):
                act.wait_ge(qk_done, t + 1)
                if not (isinstance(t, int) and t == 0):
                    act.wait_ge(phi_done, t)
                nc.scalar.activation(expo[:], b_qk[:], ACT.Exp).then_inc(er_done, 1)
                nc.scalar.activation(relu[:], b_qk[:], ACT.Relu).then_inc(er_done, 1)

            def copy_v(t, par):
                act.wait_ge(v_done, t + 1)
                if not (isinstance(t, int) and t < 2):
                    act.wait_ge(kv_done, t - 1)
                nc.scalar.activation(vext[:, par, 0:HEADS * HV].rearrange("p (h n) -> p h n", h=HEADS)[:, :, 0:HD],
                                     b_vk[:, 0:D].rearrange("p (h n) -> p h n", h=HEADS),
                                     ACT.Copy).then_inc(v_evac, 1)

            def copy_kn(t, par):
                act.wait_ge(kn_done, t + 1)
                if not (isinstance(t, int) and t < 1):
                    act.wait_ge(kv_done, t)
                nc.scalar.activation(kn[:], b_vk[:, 0:D], ACT.Copy).then_inc(kn_evac, 1)

            def split_x(t, b, i):
                act.wait_ge(xt_in[b], 16 * (i + 1))
                if not (isinstance(t, int) and t == 0):
                    act.wait_ge(v_done, t)
                nc.scalar.activation(x_part[:, 0], xt[:, b], ACT.Copy).then_inc(x_high, 1)

            def split_phi(t, par):
                act.wait_ge(phi_done, t + 1)
                if not (isinstance(t, int) and t == 0):
                    act.wait_ge(sc_done, 2 * t)
                nc.scalar.activation(k_part[:, 0], phi[:, par, 2:4], ACT.Copy).then_inc(high_done, 1)
                for e in range(2):
                    nc.scalar.activation(q_part[:, 0, :, e], phi[:, par, 0:2], ACT.Relu, scale=parity[:, e:e + 1]
                                         ).then_inc(high_done, 1)

            def copy_av(t):
                act.wait_ge(av_done, t + 1)
                if not (isinstance(t, int) and t == 0):
                    act.wait_ge(nat_done, t)
                nc.scalar.activation(avt[:].rearrange("p r n -> p (r n)"), b_av[:], ACT.Copy).then_inc(av_evac, 1)

            def copy_attT(t):
                act.wait_ge(attT_done, t + 1)
                if not (isinstance(t, int) and t == 0):
                    act.wait_ge(op_done, t)
                nc.scalar.activation(attT[:, 0].rearrange("p c n -> p (c n)"), b_tr[:, 0:D], ACT.Copy
                                     ).then_inc(attT_evac, 1)

            def copy_x1T(t):
                act.wait_ge(x1T_done, t + 1)
                if not (isinstance(t, int) and t == 0):
                    act.wait_ge(lg_done, t)
                nc.scalar.activation(x1T[:].rearrange("p c n -> p (c n)"), b_tr[:, 0:D], ACT.Copy
                                     ).then_inc(x1T_evac, 1)

            def store_p(i):
                act.wait_ge(choice, C_STEPS * i + C_PROBABLE)
                last = x1_rows.rearrange("(b i p) c -> i p b c", b=BATCH, i=BLOCKS)[bass.ds(i, 1), :, :, D:D + 1]
                nc.scalar.dma_start(last.rearrange("i p b c -> p (i b) c"),
                             top_p[:, bass.ds(i * BATCH, BATCH)].rearrange("p (b c) -> p b c", c=1),
                             allow_slow_non_contiguous=True).then_inc(p_out, 16)

            def load_w2(e, u):
                if not (isinstance(e, int) and e == 0 and u == 0):
                    act.wait_ge(w2_low_done, 4 * e + u)
                nc.scalar.dma_start(w2_raw[:].rearrange("p (c n) -> p c n", c=FC // 4),
                                    w2[bass.ds(e, 1)].rearrange("a (q c p) n -> p (a q) c n", p=P, q=4)[:, u]
                                    ).then_inc(w2_in, 16)

            def split_w2(e, u):
                act.wait_ge(w2_in, 16 * (4 * e + u + 1))
                piece = bass.ds((4 * e + u) * W2_PIECE, W2_PIECE)
                nc.scalar.activation(w2_high[:, piece], w2_raw[:], ACT.Copy
                                     ).then_inc(w2_high_done, 1)

            def exp_logits(g):
                act.wait_ge(choice, C_STEPS * g + C_SHIFTED)
                nc.scalar.activation(ex[:].rearrange("p t e -> p (t e)"),
                                     lg[:].rearrange("p t e -> p (t e)"), ACT.Exp
                                     ).then_inc(exp_done, 1)

            act.wait_ge(wvo_in, 32)
            for n, part in enumerate([wv_part, wo_part]):
                nc.scalar.activation(part[:, 0], raw[:, n], ACT.Copy).then_inc(w_high, 1)
            split_x(0, 0, 0)
            exp_relu(0)
            act.wait_ge(vec_consts, 4)
            split_phi(0, 0)
            copy_v(0, 0)
            split_x(1, 1, 0)
            copy_kn(0, 0)

            def group(i, first, last):
                for u in range(4):
                    t = 4 * i + u
                    more = not (last and u == 3)
                    load_w2(i, u)
                    if more:
                        exp_relu(t + 1)
                        copy_v(t + 1, (u + 1) % 2)
                    if not (first and u < 1):
                        copy_attT(t - 1)
                    copy_av(t)
                    if more:
                        split_phi(t + 1, (u + 1) % 2)
                    if not (first and u < 2):
                        copy_x1T(t - 2)
                    if more:
                        copy_kn(t + 1, (u + 1) % 2)
                    if not (last and u >= 2):
                        split_x(t + 2, (u + 2) % 4, i + (u + 2) // 4)
                    split_w2(i, u)
                    if u == 2 and not first:
                        exp_logits(i - 1)
                    if u == 3 and not first:
                        store_p(i - 1)

            groups(act, group)
            copy_attT(CHUNKS - 1)
            copy_x1T(CHUNKS - 2)
            copy_x1T(CHUNKS - 1)
            exp_logits(BLOCKS - 1)
            store_p(BLOCKS - 1)

            def relu_h(j, u):
                act.wait_ge(h_done, 2 * j + 1)
                act.wait_ge(w1_in[u % 2], 16 * (j // 2 + 1) if isinstance(j, int) else 8 * (j - u % 2 + 2))
                if not (isinstance(j, int) and j < 1):
                    act.wait_ge(h_low_vec, j)
                for f in range(4):
                    nc.scalar.activation(hT[:, f], [bank[0], bank[2]][u % 2][:, f * P:(f + 1) * P],
                                         ACT.Relu, bias=w1s[:, u % 2, KC * F + f:KC * F + f + 1]
                                         ).then_inc(h_act, 1)

            def copy_rows(j, u):
                act.wait_ge(xgT_done, j + 1)
                if not (isinstance(j, int) and j < 2):
                    act.wait_ge(h_done, 2 * (j - 1))
                nc.scalar.activation(xgT[:, u % 2].rearrange("p c n -> p (c n)"),
                                     [bank[6], bank[7]][u % 2][:, 0:D], ACT.Copy).then_inc(xgT_evac, 1)

            def split_h(j, u):
                for g, relued in enumerate([h_act, h_vec]):
                    act.wait_ge(relued, 4 * j + 4)
                    if g == 0 and not (isinstance(j, int) and j < 2):
                        act.wait_ge(y_done, j - 1)
                    nc.scalar.activation(hT_high[:, u % 2, 4 * g:4 * g + 4].rearrange("p f n -> p (f n)"),
                                         hT[:, 4 * g:4 * g + 4].rearrange("p f n -> p (f n)"),
                                         ACT.Copy).then_inc(h_high_done, 1)

            def step(j, u):
                if not (isinstance(j, int) and j + 1 >= TILES):
                    relu_h(j + 1, u + 1)
                if not (isinstance(j, int) and j + 2 >= TILES):
                    copy_rows(j + 2, u + 2)
                if not (isinstance(j, int) and j + 1 >= TILES):
                    split_h(j + 1, u + 1)

            copy_rows(0, 0)
            copy_rows(1, 1)
            relu_h(0, 0)
            split_h(0, 0)
            tiles(act, step)

        @block.vector
        def _(dve):
            V = nc.vector
            V.memset(vext[:], 1.0).then_inc(vec_consts, 1)
            dve.wait_ge(iotas, 3)
            V.tensor_copy(part1[:], part1_i[:]).then_inc(route, 1)
            dve.wait_ge(route, 1)
            V.tensor_scalar(lo_i[:, 0:1], part1_i[:], 1, None, ALU.subtract).then_inc(route, 1)
            dve.wait_ge(route, 2)
            V.tensor_scalar(hi_i[:, 0:1], lo_i[:, 0:1], 4, 1, ALU.logical_shift_right, ALU.bitwise_and
                            ).then_inc(route, 1)
            dve.wait_ge(route, 3)
            V.tensor_copy(parity[:, 1:2], hi_i[:, 0:1]).then_inc(vec_consts, 1)
            V.tensor_scalar(parity[:, 0:1], hi_i[:, 0:1], -1.0, 1.0, ALU.mult, ALU.add).then_inc(vec_consts, 1)
            V.memset(state[:], 0.0).then_inc(vec_consts, 1)
            V.tensor_copy(iota_p[:], iota_i[:]).then_inc(route, 1)
            V.tensor_copy(iota_b[:], iota_i[:]).then_inc(route, 1)
            V.tensor_copy(tval[:], tval_i[:]).then_inc(route, 1)
            dve.wait_ge(route, 6)
            V.tensor_scalar(rank8[:], iota_p[:, 0:E], -1.0, float(E), ALU.mult, ALU.add).then_inc(route, 1)
            V.memset(prefix_b[:, 0:E], 0.0).then_inc(route, 1)
            V.memset(tile_end[:, 0:1], 0.0).then_inc(route, 1)
            V.memset(taken[:], 0.0).then_inc(route, 1)
            dve.wait_ge(consts, 12)

            def mask_scores(t):
                dve.wait_ge(sc_done, 2 * t + 1)
                if not (isinstance(t, int) and t == 0):
                    dve.wait_ge(av_done, t)
                for n, r in enumerate(ROW_TILES[0] + ROW_TILES[1]):
                    if n == 2:
                        dve.wait_ge(sc_done, 2 * t + 2)
                    V.tensor_tensor(probs[:, r], bank[r][:].rearrange("p (j n) -> p j n", j=4),
                                    causal[:].rearrange("p (a n) -> p a n", a=1).broadcast_to([P, 4, P]),
                                    ALU.mult).then_inc(probs_done, 1)

            def phi_map(t, par):
                dve.wait_ge(er_done, 2 * t + 2)
                if not (isinstance(t, int) and t < 2):
                    dve.wait_ge(nat_done, t - 1)
                    dve.wait_ge(kn_done, t - 1)
                    dve.wait_ge(high_done, 3 * (t - 1))
                    dve.wait_ge(k_low_done, t - 1)
                V.scalar_tensor_tensor(phi[:, par].rearrange("p s n -> p (s n)"), expo[:], 1.0, relu[:],
                                       ALU.min, ALU.add).then_inc(phi_done, 1)

            def q_low(t, par):
                for e in range(2):
                    dve.wait_ge(high_done, 3 * t + 2 + e)
                    V.scalar_tensor_tensor(q_part[:, 1, :, e], phi[:, par, 0:2], parity[:, e:e + 1],
                                           q_part[:, 0, :, e].bitcast(F32), ALU.mult, ALU.subtract
                                           ).then_inc(q_low_done, 1)

            def mask_state(t):
                dve.wait_ge(kv_done, t + 1)
                if not (isinstance(t, int) and t == 0):
                    dve.wait_ge(state_done, t)
                V.tensor_tensor(state_add[:].rearrange("p c (h n) -> p c h n", h=HALF),
                                b_kv[:, 0:HEADS * HV].rearrange("p (c h n) -> p c h n", c=KC, h=HALF),
                                diag[:].rearrange("p (a h) n -> p a h n", a=1).broadcast_to([P, KC, HALF, HV]),
                                ALU.mult).then_inc(kv_masked, 1)

            def divide(t):
                dve.wait_ge(nat_done, t + 1)
                nat = b_nat[:, 0:HEADS * HV].rearrange("p (h n) -> p h n", h=HEADS)
                V.tensor_scalar(den[:], nat[:, :, HD], DEN_EPS, None, ALU.add).then_inc(den_done, 1)
                dve.wait_ge(den_done, t + 1)
                V.reciprocal(rden[:], den[:]).then_inc(rden_done, 1)
                dve.wait_ge(rden_done, t + 1)
                if not (isinstance(t, int) and t == 0):
                    dve.wait_ge(attT_done, t)
                V.tensor_tensor(att[:].rearrange("p (h n) -> p h n", h=HEADS), nat[:, :, 0:HD],
                                rden[:].rearrange("p (h a) -> p h a", a=1).broadcast_to([P, HEADS, HD]),
                                ALU.mult).then_inc(att_done, 1)

            def attT_split(t):
                dve.wait_ge(attT_evac, t + 1)
                V.tensor_tensor(attT[:, 1].rearrange("p c n -> p (c n)"), b_tr[:, 0:D],
                                attT[:, 0].rearrange("p c n -> p (c n)").bitcast(F32), ALU.subtract
                                ).then_inc(attT_low, 1)

            def residual(t, b, i, par):
                dve.wait_ge(op_done, t + 1)
                dve.wait_ge(xn_in[b], 16 * (i + 1))
                V.tensor_tensor(z[:, par], b_op[:, 0:D], xn[:, b], ALU.add).then_inc(z_done, 1)
                dve.wait_ge(z_done, t + 1)
                V.bn_stats(stats[:], z[:, par]).then_inc(stats_done, 1)
                dve.wait_ge(consts, 12)
                dve.wait_ge(stats_done, t + 1)
                V.bn_aggr(mv[:, par], stats[:]).then_inc(mv_done, 1)

            def normalise(t, b, i, par):
                dve.wait_ge(rstd_done, t + 1)
                dve.wait_ge(mv_done, t + 1)
                if not (isinstance(t, int) and t < 4):
                    dve.wait_ge(x1_out[b], 16 * i)
                    dve.wait_ge(x1T_done, t - 2)
                V.tensor_scalar(x1[:, b], z[:, par], mv[:, par, 0:1], rstd[:, par:par + 1],
                                ALU.subtract, ALU.mult).then_inc(x1_done, 1)

            def over_e4(ap):
                return ap.rearrange("p (t a) -> p t a", a=1).broadcast_to([P, 4, E])

            def over_t4(ap):
                return ap.rearrange("p (a e) -> p a e", a=1).broadcast_to([P, 4, E])

            def choose(g, n):
                tt = bass.ds(4 * g, 4)
                if n > 1:
                    dve.wait_ge(choice, C_STEPS * g + n - 1)
                if n == 1:
                    dve.wait_ge(lg_done, 4 * g + 4)
                    V.tensor_tensor(lg[:], b_lg[:, bass.ds(4 * E * g, 4 * E)]
                                    .rearrange("p (t e) -> p t e", t=4), over_t4(bg[:]), ALU.add
                                    ).then_inc(choice, 1)
                elif n == 2:
                    V.tensor_reduce(lmax[:], lg[:], AX_X, ALU.max).then_inc(choice, 1)
                elif n == 3:
                    V.tensor_tensor(lg[:], lg[:], over_e4(lmax[:]), ALU.subtract).then_inc(choice, 1)
                elif n == 4:
                    V.scalar_tensor_tensor(hit[:], lg[:], 0.0, over_t4(rank8[:]), ALU.is_ge, ALU.mult
                                           ).then_inc(choice, 1)
                elif n == 5:
                    V.tensor_reduce(first_hit[:], hit[:], AX_X, ALU.max).then_inc(choice, 1)
                elif n == 8:
                    V.tensor_tensor(onehot[:], hit[:], over_e4(first_hit[:]), ALU.is_equal
                                    ).then_inc(choice, 1)
                elif n == 9:
                    V.tensor_copy(onehot_b[:, bass.ds(4 * E * g, 4 * E)],
                                  onehot[:].rearrange("p t e -> p (t e)")).then_inc(choice, 1)
                elif n >= 10:
                    at = E * (4 * g + n - 10)
                    V.tensor_tensor(prefix_b[:, bass.ds(at + E, E)], prefix_b[:, bass.ds(at, E)],
                                    onehot_b[:, bass.ds(at, E)], ALU.add).then_inc(choice, 1)
                elif n == 6:
                    dve.wait_ge(exp_done, g + 1)
                    V.tensor_reduce(esum[:], ex[:], AX_X, ALU.add).then_inc(choice, 1)
                elif n == 7:
                    V.reciprocal(top_p[:, tt], esum[:]).then_inc(choice, 1)

            for n, part in enumerate([wv_part, wo_part]):
                dve.wait_ge(w_high, n + 1)
                V.tensor_tensor(part[:, 1], raw[:, n], part[:, 0].bitcast(F32), ALU.subtract).then_inc(w_low, 1)

            def wide(ap, n):
                return ap.rearrange("p (t a) -> p t a", a=1).broadcast_to([P, ap.shape[-1], n])

            def deep(ap, n):
                return ap.rearrange("p (a e) -> p a e", a=1).broadcast_to([P, n, ap.shape[-1]])

            chosen = onehot_b[:].rearrange("p (t e) -> p t e", e=E)
            eg, ee, en = slice(0, EARLY), EARLY * E, EARLY_TILES
            rank = b_lg[:, 264:264 + ee].rearrange("p (t e) -> p t e", t=EARLY)
            last_end = tile_end[:, 1:1 + E]

            def early_step(n):
                if n > 0:
                    dve.wait_ge(early, n)
                if n == 0:
                    dve.wait_ge(early_counted, 1)
                    V.tensor_copy(count_i[:], b_lg[:, 256:256 + E]).then_inc(early, 1)
                elif n == 1:
                    V.tensor_scalar(tiles_i[:], count_i[:], 7, None, ALU.logical_shift_right).then_inc(early, 1)
                elif n == 2:
                    V.tensor_copy(ntile[:], tiles_i[:]).then_inc(early, 1)
                elif n == 3:
                    V.tensor_tensor_scan(last_end, ones_e[:], ntile[:], 0.0, ALU.mult, ALU.add
                                   ).then_inc(early, 1)
                elif n == 4:
                    V.tensor_scalar(last_end, last_end, float(EARLY_TILES), None, ALU.min).then_inc(early, 1)
                elif n == 5:
                    V.scalar_tensor_tensor(early_pick[:], deep(tile_end[:, 0:E], EARLY), float(P), rank,
                                           ALU.mult, ALU.add).then_inc(early, 1)
                elif n == 6:
                    V.tensor_tensor(early_pick[:], early_pick[:], chosen[:, eg], ALU.mult).then_inc(early, 1)
                elif n == 7:
                    V.tensor_reduce(slot[:, eg], early_pick[:], AX_X, ALU.add).then_inc(early, 1)
                elif n == 8:
                    V.tensor_tensor(early_pick[:], deep(last_end, EARLY), chosen[:, eg], ALU.mult
                                   ).then_inc(early, 1)
                elif n == 9:
                    V.tensor_reduce(early_limit[:], early_pick[:], AX_X, ALU.add).then_inc(early, 1)
                elif n == 10:
                    V.tensor_copy(slot_i[:, eg], slot[:, eg]).then_inc(early, 1)
                elif n == 11:
                    V.tensor_scalar(lo_i[:, eg], slot_i[:, eg], P - 1, None, ALU.bitwise_and).then_inc(early, 1)
                elif n == 12:
                    V.tensor_copy(lo[:, eg], lo_i[:, eg]).then_inc(early, 1)
                elif n == 13:
                    V.tensor_scalar(hi_i[:, eg], slot_i[:, eg], 7, None, ALU.logical_shift_right
                                   ).then_inc(early, 1)
                elif n == 14:
                    V.tensor_copy(hi[:, eg], hi_i[:, eg]).then_inc(early, 1)
                elif n == 15:
                    V.tensor_tensor(taken[:, eg], hi[:, eg], early_limit[:], ALU.is_lt).then_inc(early, 1)
                elif n == 16:
                    V.tensor_tensor(early_limit[:], hi[:, eg], early_limit[:], ALU.is_ge).then_inc(early, 1)
                elif n == 17:
                    V.scalar_tensor_tensor(hi[:, eg], early_limit[:], float(P), hi[:, eg], ALU.mult, ALU.add
                                   ).then_inc(early, 1)
                elif n == 18:
                    V.tensor_tensor(early_hi_hot[:], deep(iota_p[:, 0:en], EARLY), wide(hi[:, eg], en), ALU.is_equal
                                   ).then_inc(early, 1)
                elif n == 19:
                    V.tensor_scalar(early_mov[:, :, 0], early_hi_hot[:], part1[:], None, ALU.mult
                                   ).then_inc(early, 1)
                elif n == 20:
                    V.tensor_tensor(early_mov[:, :, 1], early_hi_hot[:], wide(tval[:, eg], en), ALU.mult
                                   ).then_inc(early, 1)
                elif n == 21:
                    V.tensor_tensor(early_n[:], last_end, tile_end[:, 0:E], ALU.subtract).then_inc(early, 1)
                elif n == 22:
                    V.tensor_tensor(early_ended, wide(iota_p[:, 0:en], E), deep(last_end, en), ALU.is_ge
                                   ).then_inc(early, 1)
                elif n == 23:
                    V.tensor_reduce(expert_f[:, 0:en], early_ended, AX_X, ALU.add).then_inc(early, 1)

            def early_work(u, n):
                k = 5 * u + n - 1
                per = [2, 2, 2, 2, 2] + [3, 3, 3, 3, 2]
                if k < 10:
                    for m in range(sum(per[:k]), sum(per[:k + 1])):
                        early_step(m)
                else:
                    if k == 10:
                        dve.wait_ge(early, EARLY_STEPS)
                        V.tensor_copy(expert_i[:, 0:en], expert_f[:, 0:en]).then_inc(experts_ready, 1)
                    half = (k - 10) // 5
                    if k == 15:
                        dve.wait_ge(early_half, 1)
                        V.tensor_copy(early_slots[:].rearrange("p a n -> p (a n)"), early_sums[0]).then_inc(early, 1)
                    for m in range(2):
                        t = 10 * half + 2 * (n - 1) + m
                        V.tensor_scalar(early_lo_hot[:, t % 10], iota_b[:], lo[:, t:t + 1], None, ALU.is_equal
                                        ).then_inc(early_lo, 1)

            phi_map(0, 0)
            q_low(0, 0)

            def group(i, first, last):
                for u in range(4):
                    t, par = 4 * i + u, u % 2

                    def choose_after(n):
                        if u >= 2 and not first:
                            for m in CHOICE_AT[u - 2][n - 1]:
                                choose(i - 1, m)
                        if last:
                            early_work(u, n)

                    choose_after(1)
                    mask_scores(t)
                    choose_after(2)
                    if not (last and u == 3):
                        phi_map(t + 1, (u + 1) % 2)
                    if not (first and u < 1):
                        attT_split(t - 1)
                    choose_after(3)
                    if not (first and u < 2):
                        normalise(t - 2, (u + 2) % 4, i + (u + 2) // 4 - 1, par)
                    choose_after(4)
                    mask_state(t)
                    if not (last and u == 3):
                        q_low(t + 1, (u + 1) % 2)
                    choose_after(5)
                    divide(t)
                    if not (first and u < 1):
                        residual(t - 1, (u + 3) % 4, i + (u + 3) // 4 - 1, (u + 1) % 2)

            groups(dve, group)
            dve.wait_ge(early_half, 2)
            dve.wait_ge(early, EARLY_STEPS + 1)
            V.tensor_tensor(early_slots[:].rearrange("p a n -> p (a n)"),
                            early_slots[:].rearrange("p a n -> p (a n)"),
                            early_sums[1], ALU.add).then_inc(early_done, 1)
            attT_split(CHUNKS - 1)
            normalise(CHUNKS - 2, 2, BLOCKS - 1, 0)
            residual(CHUNKS - 1, 3, BLOCKS - 1, 1)
            dve.wait_ge(early_done, 1)
            V.scalar_tensor_tensor(tok1[:, 0:en], early_slots[:, 1], float(P), early_slots[:, 0], ALU.mult, ALU.add
                                   ).then_inc(early_done, 1)
            dve.wait_ge(early_done, 2)
            V.tensor_scalar(gather_f[:, 0:en], tok1[:, 0:en], -1.0, None, ALU.add).then_inc(early_done, 1)
            dve.wait_ge(early_done, 3)
            V.tensor_copy(gather_i[:, 0:en], gather_f[:, 0:en]).then_inc(early_done, 1)
            V.tensor_copy(scatter_i[:, 0:en], gather_f[:, 0:en]).then_inc(early_done, 1)
            dve.wait_ge(early_done, 5)
            for j in range(4):
                V.tensor_copy(gidx[:, j:j + 1], gather_i[:, j:j + 1]).then_inc(first_gidx, 1)
            normalise(CHUNKS - 1, 3, BLOCKS - 1, 1)

            for n in range(1, C_STEPS + 1):
                choose(BLOCKS - 1, n)

            ln = LATE_TILES
            ranks = bank[5][:, 0:CHUNKS * E].rearrange("p (t e) -> p t e", t=CHUNKS)

            def late_step(n):
                if n < 20:
                    dve.wait_ge(route, R_COUNTS + n)
                elif n < 22:
                    dve.wait_ge(route, R_COUNTS + n - 1)
                if n == 0:
                    V.tensor_scalar(tiles_i[:], count_i[:], 7, None, ALU.logical_shift_right).then_inc(route, 1)
                elif n == 1:
                    V.tensor_copy(ntile[:], tiles_i[:]).then_inc(route, 1)
                elif n == 2:
                    V.tensor_tensor(ntile[:], ntile[:], early_n[:], ALU.subtract).then_inc(route, 1)
                elif n == 3:
                    V.tensor_tensor_scan(tend[:], ones_e[:], ntile[:], 0.0, ALU.mult, ALU.add
                                   ).then_inc(route, 1)
                elif n == 4:
                    V.tensor_tensor(tstart[:], tend[:], ntile[:], ALU.subtract).then_inc(route, 1)
                elif n == 5:
                    V.tensor_tensor(shift[:], tstart[:], early_n[:], ALU.subtract).then_inc(route, 1)
                elif n == 6:
                    dve.wait_ge(rank_read, 1)
                    V.tensor_reduce(slot[:], pick[:], AX_X, ALU.add).then_inc(route, 1)
                elif n == 7:
                    V.tensor_tensor(pick[:], deep(shift[:], CHUNKS), chosen, ALU.mult).then_inc(route, 1)
                elif n == 8:
                    V.tensor_reduce(offset[:], pick[:], AX_X, ALU.add).then_inc(route, 1)
                elif n == 9:
                    V.tensor_copy(slot_i[:], slot[:]).then_inc(route, 1)
                elif n == 10:
                    V.tensor_scalar(lo_i[:], slot_i[:], P - 1, None, ALU.bitwise_and).then_inc(route, 1)
                elif n == 11:
                    V.tensor_copy(lo[:], lo_i[:]).then_inc(route, 1)
                elif n == 12:
                    V.tensor_scalar(hi_i[:], slot_i[:], 7, None, ALU.logical_shift_right).then_inc(route, 1)
                elif n == 13:
                    V.tensor_copy(hi[:], hi_i[:]).then_inc(route, 1)
                elif n == 14:
                    V.tensor_tensor(hi[:], hi[:], offset[:], ALU.add).then_inc(route, 1)
                elif n == 15:
                    V.scalar_tensor_tensor(hi[:], taken[:], float(P), hi[:], ALU.mult, ALU.add
                                   ).then_inc(route, 1)
                elif n == 16:
                    V.tensor_tensor(ended[:], wide(iota_p[:, 0:ln], E), deep(tend[:], ln), ALU.is_ge
                                   ).then_inc(route, 1)
                elif n == 17:
                    V.tensor_reduce(expert_f[:, en:], ended[:], AX_X, ALU.add).then_inc(route, 1)
                elif n == 18:
                    V.tensor_scalar(expert_f[:, en:], expert_f[:, en:], float(E - 1), None, ALU.min
                                   ).then_inc(route, 1)
                elif n == 19:
                    V.tensor_copy(expert_i[:, en:], expert_f[:, en:]).then_inc(experts_ready, 1)
                elif n == 20:
                    V.tensor_tensor(hi_hot[:], deep(iota_p[:, 0:ln], CHUNKS), wide(hi[:], ln), ALU.is_equal
                                   ).then_inc(route, 1)
                elif n == 21:
                    V.tensor_scalar(mov[:, :, 0], hi_hot[:], part1[:], None, ALU.mult).then_inc(mov_done, 1)
                elif n == 22:
                    V.tensor_tensor(mov[:, :, 1], hi_hot[:], wide(tval[:], ln), ALU.mult).then_inc(mov_done, 1)
                else:
                    t = n - 23
                    V.tensor_scalar(lo_hot[:, t], iota_b[:], lo[:, t:t + 1], None, ALU.is_equal
                                    ).then_inc(lo_hot_done, 1)

            def late_work(j, part):
                if part == 1 and j == 0:
                    dve.wait_ge(count_done, 1)
                    V.tensor_scalar(count_i[:], bank[5][:, 256:256 + E], float(P - 1), None, ALU.add).then_inc(route, 1)
                    V.tensor_tensor(pick[:], ranks, chosen, ALU.mult).then_inc(rank_read, 1)
                elif 1 <= j < TABLE_STEP:
                    piece_no = 2 * (j - 1) + part
                    each = -(-LATE_STEPS // (2 * (TABLE_STEP - 1)))
                    for m in range(each * piece_no, min(each * (piece_no + 1), LATE_STEPS)):
                        late_step(m)
                elif part == 1 and j == TABLE_STEP:
                    dve.wait_ge(slots_done, 1)
                    V.tensor_copy(slot_sb[:].rearrange("p a n -> p (a n)"), bank[5][:, 0:2 * ln]).then_inc(slots_read, 1)
                    dve.wait_ge(slots_read, 1)
                    V.scalar_tensor_tensor(tok1[:, en:], slot_sb[:, 1], float(P), slot_sb[:, 0], ALU.mult, ALU.add
                                    ).then_inc(route, 1)
                    dve.wait_ge(route, R_FOUND + 1)
                    V.tensor_scalar(gather_f[:, en:], tok1[:, en:], -1.0, 0.0, ALU.add, ALU.max).then_inc(route, 1)
                    dve.wait_ge(route, R_FOUND + 2)
                    V.tensor_copy(gather_i[:, en:], gather_f[:, en:]).then_inc(route, 1)
                    dve.wait_ge(route, R_FOUND + 3)
                    V.tensor_scalar(scatter_f[:], tok1[:, en:], 0.0, float(2 * TOKENS), ALU.is_equal, ALU.mult
                                    ).then_inc(route, 1)
                    dve.wait_ge(route, R_FOUND + 4)
                    V.scalar_tensor_tensor(scatter_f[:], tok1[:, en:], -1.0, scatter_f[:], ALU.add, ALU.add
                                    ).then_inc(route, 1)
                    dve.wait_ge(route, R_FOUND + 5)
                    V.tensor_copy(scatter_i[:, en:], scatter_f[:]).then_inc(route, 1)
                    dve.wait_ge(route, R_FOUND + 6)

            def next_index(j, u):
                dve.wait_ge(xg_in[u % 4], 16 * (j // 4) if isinstance(j, int) else 4 * (j - u % 4))
                V.tensor_copy(gidx[:, u % 4:u % 4 + 1], gather_i[:, bass.ds(j, 1)]).then_inc(gidx_done, 1)

            def relu_h(j, u):
                dve.wait_ge(h_done, 2 * j + 2)
                dve.wait_ge(w1_in[u % 2], 16 * (j // 2 + 1) if isinstance(j, int) else 8 * (j - u % 2 + 2))
                if not (isinstance(j, int) and j < 1):
                    dve.wait_ge(h_low_pool, j)
                for f in range(4, FC):
                    V.tensor_scalar(hT[:, f], [bank[1], bank[3]][u % 2][:, (f - 4) * P:(f - 3) * P],
                                    w1s[:, u % 2, KC * F + f:KC * F + f + 1], 0.0, ALU.add, ALU.max
                                    ).then_inc(h_vec, 1)

            def finish(j, u):
                dve.wait_ge(y_done, j + 1)
                dve.wait_ge(b2_in[u % 4], 16 * (j // 4 + 1) if isinstance(j, int) else 4 * (j - u % 4 + 4))
                V.tensor_tensor(z2[:, u % 2], [bank[4], bank[5]][u % 2][:, 0:D], b2s[:, u % 4], ALU.add
                                ).then_inc(yb_done, 1)
                dve.wait_ge(yb_done, j + 1)
                dve.wait_ge(xg_in[u % 4], 16 * (j // 4 + 1) if isinstance(j, int) else 4 * (j - u % 4 + 4))
                V.scalar_tensor_tensor(z2[:, u % 2], z2[:, u % 2], xg[:, u % 4, D:D + 1], xg[:, u % 4, 0:D],
                                       ALU.mult, ALU.add).then_inc(z2_done, 1)
                dve.wait_ge(z2_done, j + 1)
                V.bn_stats(stats2[:], z2[:, u % 2]).then_inc(stats2_done, 1)
                dve.wait_ge(consts, 12)
                dve.wait_ge(stats2_done, j + 1)
                V.bn_aggr(mv2[:, u % 2], stats2[:]).then_inc(mv2_done, 1)

            def normalise2(j, u):
                dve.wait_ge(rstd2_done, j + 1)
                dve.wait_ge(mv2_done, j + 1)
                if not (isinstance(j, int) and j < 2):
                    dve.wait_ge(y_out[u % 2], 16 * (j // 2) if isinstance(j, int) else 8 * (j - u % 2))
                V.tensor_copy(sidx[:, u % 2:u % 2 + 1], scatter_i[:, bass.ds(j, 1)]).then_inc(sidx_done, 1)
                V.tensor_scalar(yo[:, u % 2], z2[:, u % 2], mv2[:, u % 2, 0:1], rstd2[:, u % 2:u % 2 + 1],
                                ALU.subtract, ALU.mult).then_inc(yo_done, 1)

            def split_h(j, u):
                dve.wait_ge(h_high_done, 2 * j + 1)
                V.tensor_tensor(hT_low[:, u % 2, 0:4].rearrange("p f n -> p (f n)"),
                                hT[:, 0:4].rearrange("p f n -> p (f n)"),
                                hT_high[:, u % 2, 0:4].rearrange("p f n -> p (f n)").bitcast(F32),
                                ALU.subtract).then_inc(h_low_vec, 1)

            relu_h(0, 0)
            split_h(0, 0)

            def step(j, u):
                if not (isinstance(j, int) and j + 1 >= TILES):
                    relu_h(j + 1, u + 1)
                if not (isinstance(j, int) and j + 4 >= TILES):
                    next_index(j + 4, u)
                if not (isinstance(j, int) and j + 1 >= TILES):
                    split_h(j + 1, u + 1)
                if isinstance(j, int) and j < STRAIGHT:
                    late_work(j, 0)
                finish(j, u)
                if isinstance(j, int) and j < STRAIGHT:
                    late_work(j, 1)
                normalise2(j, u)

            tiles(dve, step, STRAIGHT)


def kernel(**inputs):
    import numpy as np
    import concourse.bacc as bacc
    from concourse.bass_utils import run_bass_kernel_spmd as run

    x = np.ascontiguousarray(inputs["L0_attn_x"])
    w1 = np.asarray(inputs["L0_ffn_W1"])
    b1 = np.asarray(inputs["L0_ffn_b1"])
    arrays = {
        "x": x,
        "xT": np.ascontiguousarray(x.reshape(BATCH, BLOCKS, P, KC, P).transpose(1, 0, 4, 3, 2)),
        "w_qkv": np.ascontiguousarray(inputs["L0_attn_W_qkv"]),
        "w_out": np.ascontiguousarray(inputs["L0_attn_W_out"]),
        "w_gate": np.ascontiguousarray(inputs["L0_ffn_w_gate"]),
        "b_gate": np.ascontiguousarray(inputs["L0_ffn_b_gate"]),
        "w1b": np.ascontiguousarray(np.concatenate([
            w1.reshape(E, KC, P, F).transpose(0, 2, 1, 3).reshape(E, P, KC * F),
            b1.reshape(E, FC, P).transpose(0, 2, 1)], axis=2)),
        "w2": np.ascontiguousarray(inputs["L0_ffn_W2"]),
        "b2": np.ascontiguousarray(inputs["L0_ffn_b2"]),
    }
    nc = bacc.Bacc("TRN2", target_bir_lowering=False, num_devices=1)
    args = [nc.dram_tensor(n, a.shape, mybir.dt.from_np(a.dtype), kind="ExternalInput").ap()
            for n, a in arrays.items()]
    out = nc.dram_tensor("out", (BATCH, SEQ, D), F32, kind="ExternalOutput").ap()
    attention_moe(nc, *args, out)
    r = run(nc, [arrays], core_ids=[0])
    return r.results[0]["out"]
```
